# Optimizing a Trainium2 kernel written in Bass

```python
import numpy as np
import jax
import jax.numpy as jnp

def _softmax(x, axis=-1):
    return jax.nn.softmax(x, axis=axis)

def _gelu(x):
    return jax.nn.gelu(x, approximate=True)

def _silu(x):
    return jax.nn.silu(x)

def _sigmoid(x):
    return jax.nn.sigmoid(x)

def _layernorm(x, axis=-1, eps=1e-05):
    m = jnp.mean(x, axis=axis, keepdims=True)
    v = jnp.var(x, axis=axis, keepdims=True)
    return (x - m) / jnp.sqrt(v + eps)

def _scatter_add(tgt, idx, src, axis=0):
    return tgt.at[idx].add(src)

def _segment_sum(src, seg, n):
    return jax.ops.segment_sum(src, seg, n)
kernel_name = 'mk_prb_d1_jaxref_r8_3a6730'

def setup_inputs(seed: int=0):
    np.random.seed(seed)
    _w = jnp.asarray

    def _L0_attn_setup():
        import math
        import jax, jax.numpy as jnp
        import numpy as np
        B, T, D, H = (4, 128, 128, 8)
        HD = D // H

        def _trigram_dirs():
            t = np.array([[(i >> b & 1) * 2 - 1 for b in (2, 1, 0)] for i in range(8)], dtype=np.float32)
            return jnp.asarray(t / np.linalg.norm(t, axis=1, keepdims=True))
        key = jax.random.key(seed)
        k1, k2, k3, k4 = jax.random.split(key, 4)
        x = jax.random.normal(k1, (B, T, D), dtype=jnp.float32)
        Wqkv = jax.random.normal(k2, (D, 3 * D), dtype=jnp.float32) * 0.02
        Wout = jax.random.normal(k3, (D, D), dtype=jnp.float32) * 0.02
        head_scales = jax.random.normal(k4, (H,), dtype=jnp.float32) * 0.1
        head_dirs = _trigram_dirs()
        return {'x': x, 'Wqkv': Wqkv, 'Wout': Wout, 'head_scales': head_scales, 'head_dirs': head_dirs}
    _L0_attn_in = _L0_attn_setup()

    def _L0_ffn_setup():
        import jax, jax.numpy as jnp
        import numpy as np
        DIM = 128
        DEPTH = 2
        HEADS = 8
        DIM_HEAD = 64
        WINDOW = 64
        INNER = HEADS * DIM_HEAD
        HID = int(DIM * 4 * 2 / 3)
        B, N = (2, 1024)
        QK_SCALE = 8.0

        def shift_token(t):
            t1, t2 = jnp.split(t, 2, axis=-1)
            t2 = jnp.pad(t2, ((0, 0), (1, 0), (0, 0)))[:, :-1]
            return jnp.concatenate([t1, t2], axis=-1)

        def l2norm(t):
            return t / jnp.clip(jnp.linalg.norm(t, axis=-1, keepdims=True), 1e-12)

        def rotate_half(x):
            x1, x2 = jnp.split(x, 2, axis=-1)
            return jnp.concatenate([-x2, x1], axis=-1)

        def rotary_xpos(q, k):
            n = q.shape[-2]
            half_idx = jnp.arange(0, DIM_HEAD, 2, dtype=jnp.float32)
            inv_freq = 1.0 / 10000.0 ** (half_idx / DIM_HEAD)
            t = jnp.arange(n, dtype=jnp.float32)
            freqs = t[:, None] * inv_freq[None, :]
            freqs = jnp.concatenate([freqs, freqs], axis=-1)
            base = (half_idx + 0.4 * DIM_HEAD) / (1.4 * DIM_HEAD)
            power = (t - n // 2) / float(WINDOW // 2)
            scale = base[None, :] ** power[:, None]
            scale = jnp.concatenate([scale, scale], axis=-1)
            cos, sin = (jnp.cos(freqs), jnp.sin(freqs))
            q = q * cos * scale + rotate_half(q) * sin * scale
            k = k * cos / scale + rotate_half(k) * sin / scale
            return (q, k)

        def local_attention(q, k, v):
            b, h, n, d = q.shape
            w = n // WINDOW
            bq = q.reshape(b, h, w, WINDOW, d) * QK_SCALE
            bk = k.reshape(b, h, w, WINDOW, d)
            bv = v.reshape(b, h, w, WINDOW, d)

            def look_around(t):
                p = jnp.pad(t, ((0, 0), (0, 0), (1, 0), (0, 0), (0, 0)))
                return jnp.concatenate([p[:, :, :w], p[:, :, 1:]], axis=3)
            bk, bv = (look_around(bk), look_around(bv))
            bt = jnp.arange(n).reshape(w, WINDOW)
            btp = jnp.pad(bt, ((1, 0), (0, 0)), constant_values=-1)
            btk = jnp.concatenate([btp[:w], btp[1:]], axis=1)
            sim = jnp.einsum('bhwid,bhwjd->bhwij', bq, bk)
            i = bt[:, :, None]
            j = btk[:, None, :]
            mask = (i < j) | (i > j + WINDOW) | (j == -1)
            sim = jnp.where(mask, -jnp.finfo(sim.dtype).max, sim)
            attn = jax.nn.softmax(sim, axis=-1)
            out = jnp.einsum('bhwij,bhwjd->bhwid', attn, bv)
            return out.reshape(b, h, n, d)

        def _layer(x, wqkv, qs, ksc, wo, lg, lb, w1, b1, w2, b2):
            b, n, _ = x.shape
            h = shift_token(x)
            qkv = h @ wqkv
            q, k, v = jnp.split(qkv, 3, axis=-1)
            to_heads = lambda t: t.reshape(b, n, HEADS, DIM_HEAD).transpose(0, 2, 1, 3)
            q, k, v = (to_heads(q), to_heads(k), to_heads(v))
            q = l2norm(q) * qs
            k = l2norm(k) * ksc
            q, k = rotary_xpos(q, k)
            o = local_attention(q, k, v)
            o = o.transpose(0, 2, 1, 3).reshape(b, n, INNER)
            x = x + o @ wo
            h = shift_token(x)
            mu = h.mean(-1, keepdims=True)
            var = h.var(-1, keepdims=True)
            h = (h - mu) / jnp.sqrt(var + 1e-05) * lg + lb
            h = h @ w1 + b1
            a, g = jnp.split(h, 2, axis=-1)
            h = a * jax.nn.gelu(g, approximate=False)
            x = x + h @ w2 + b2
            return x
        key = jax.random.key(seed)
        ks = jax.random.split(key, 6)
        return {'x': jax.random.normal(ks[0], (B, N, DIM), jnp.float32), 'wqkv': jax.random.normal(ks[1], (DEPTH, DIM, 3 * INNER), jnp.float32) * 0.02, 'q_scale': jnp.ones((DEPTH, DIM_HEAD), jnp.float32), 'k_scale': jnp.ones((DEPTH, DIM_HEAD), jnp.float32), 'wo': jax.random.normal(ks[2], (DEPTH, INNER, DIM), jnp.float32) * 0.02, 'ln_g': jnp.ones((DEPTH, DIM), jnp.float32), 'ln_b': jnp.zeros((DEPTH, DIM), jnp.float32), 'w1': jax.random.normal(ks[3], (DEPTH, DIM, 2 * HID), jnp.float32) * 0.02, 'b1': jnp.zeros((DEPTH, 2 * HID), jnp.float32), 'w2': jax.random.normal(ks[4], (DEPTH, HID, DIM), jnp.float32) * 0.02, 'b2': jnp.zeros((DEPTH, DIM), jnp.float32)}
    _L0_ffn_in = _L0_ffn_setup()
    _d = {'L0_attn_x': _L0_attn_in['x'], 'L0_attn_Wqkv': _L0_attn_in['Wqkv'], 'L0_attn_Wout': _L0_attn_in['Wout'], 'L0_attn_head_scales': _L0_attn_in['head_scales'], 'L0_attn_head_dirs': _L0_attn_in['head_dirs'], 'L0_ffn_wqkv': _L0_ffn_in['wqkv'], 'L0_ffn_q_scale': _L0_ffn_in['q_scale'], 'L0_ffn_k_scale': _L0_ffn_in['k_scale'], 'L0_ffn_wo': _L0_ffn_in['wo'], 'L0_ffn_ln_g': _L0_ffn_in['ln_g'], 'L0_ffn_ln_b': _L0_ffn_in['ln_b'], 'L0_ffn_w1': _L0_ffn_in['w1'], 'L0_ffn_b1': _L0_ffn_in['b1'], 'L0_ffn_w2': _L0_ffn_in['w2'], 'L0_ffn_b2': _L0_ffn_in['b2']}
    _x0 = _d['L0_attn_x']
    _d['L0_attn_x'] = jax.random.normal(jax.random.fold_in(jax.random.key(seed), 1), (4, 512, 128), dtype=_x0.dtype)
    del _x0
    return _d

def reference(L0_attn_x, L0_attn_Wqkv, L0_attn_Wout, L0_attn_head_scales, L0_attn_head_dirs, L0_ffn_wqkv, L0_ffn_q_scale, L0_ffn_k_scale, L0_ffn_wo, L0_ffn_ln_g, L0_ffn_ln_b, L0_ffn_w1, L0_ffn_b1, L0_ffn_w2, L0_ffn_b2):

    def _L0_attn_ref(x, Wqkv, Wout, head_scales, head_dirs):
        import math
        import jax, jax.numpy as jnp
        import numpy as np
        B, T, D, H = (4, 128, 128, 8)
        HD = D // H

        def _trigram_dirs():
            t = np.array([[(i >> b & 1) * 2 - 1 for b in (2, 1, 0)] for i in range(8)], dtype=np.float32)
            return jnp.asarray(t / np.linalg.norm(t, axis=1, keepdims=True))
        b, t, d = x.shape
        scale = 1.0 / math.sqrt(HD)
        qkv = (x @ Wqkv).reshape(b, t, 3, H, HD)
        qkv = jnp.transpose(qkv, (2, 0, 3, 1, 4))
        q, k, v = (qkv[0], qkv[1], qkv[2])
        scores = jnp.einsum('bhqd,bhkd->bhqk', q, k) * scale
        q_proj = jnp.einsum('bhtd,hd->bht', q[..., :3], head_dirs)
        k_proj = jnp.einsum('bhtd,hd->bht', k[..., :3], head_dirs)
        geo_bias = q_proj[..., :, None] * k_proj[..., None, :]
        scores = scores + head_scales[None, :, None, None] * geo_bias
        causal = jnp.tril(jnp.ones((t, t), dtype=bool))
        scores = jnp.where(causal, scores, -jnp.inf)
        attn = jax.nn.softmax(scores, axis=-1)
        out = jnp.einsum('bhqk,bhkd->bhqd', attn, v)
        out = jnp.transpose(out, (0, 2, 1, 3)).reshape(b, t, d)
        return out @ Wout

    def _L0_ffn_ref(x, wqkv, q_scale, k_scale, wo, ln_g, ln_b, w1, b1, w2, b2):
        import jax, jax.numpy as jnp
        import numpy as np
        DIM = 128
        DEPTH = 2
        HEADS = 8
        DIM_HEAD = 64
        WINDOW = 64
        INNER = HEADS * DIM_HEAD
        HID = int(DIM * 4 * 2 / 3)
        B, N = (2, 1024)
        QK_SCALE = 8.0

        def shift_token(t):
            t1, t2 = jnp.split(t, 2, axis=-1)
            t2 = jnp.pad(t2, ((0, 0), (1, 0), (0, 0)))[:, :-1]
            return jnp.concatenate([t1, t2], axis=-1)

        def l2norm(t):
            return t / jnp.clip(jnp.linalg.norm(t, axis=-1, keepdims=True), 1e-12)

        def rotate_half(x):
            x1, x2 = jnp.split(x, 2, axis=-1)
            return jnp.concatenate([-x2, x1], axis=-1)

        def rotary_xpos(q, k):
            n = q.shape[-2]
            half_idx = jnp.arange(0, DIM_HEAD, 2, dtype=jnp.float32)
            inv_freq = 1.0 / 10000.0 ** (half_idx / DIM_HEAD)
            t = jnp.arange(n, dtype=jnp.float32)
            freqs = t[:, None] * inv_freq[None, :]
            freqs = jnp.concatenate([freqs, freqs], axis=-1)
            base = (half_idx + 0.4 * DIM_HEAD) / (1.4 * DIM_HEAD)
            power = (t - n // 2) / float(WINDOW // 2)
            scale = base[None, :] ** power[:, None]
            scale = jnp.concatenate([scale, scale], axis=-1)
            cos, sin = (jnp.cos(freqs), jnp.sin(freqs))
            q = q * cos * scale + rotate_half(q) * sin * scale
            k = k * cos / scale + rotate_half(k) * sin / scale
            return (q, k)

        def local_attention(q, k, v):
            b, h, n, d = q.shape
            w = n // WINDOW
            bq = q.reshape(b, h, w, WINDOW, d) * QK_SCALE
            bk = k.reshape(b, h, w, WINDOW, d)
            bv = v.reshape(b, h, w, WINDOW, d)

            def look_around(t):
                p = jnp.pad(t, ((0, 0), (0, 0), (1, 0), (0, 0), (0, 0)))
                return jnp.concatenate([p[:, :, :w], p[:, :, 1:]], axis=3)
            bk, bv = (look_around(bk), look_around(bv))
            bt = jnp.arange(n).reshape(w, WINDOW)
            btp = jnp.pad(bt, ((1, 0), (0, 0)), constant_values=-1)
            btk = jnp.concatenate([btp[:w], btp[1:]], axis=1)
            sim = jnp.einsum('bhwid,bhwjd->bhwij', bq, bk)
            i = bt[:, :, None]
            j = btk[:, None, :]
            mask = (i < j) | (i > j + WINDOW) | (j == -1)
            sim = jnp.where(mask, -jnp.finfo(sim.dtype).max, sim)
            attn = jax.nn.softmax(sim, axis=-1)
            out = jnp.einsum('bhwij,bhwjd->bhwid', attn, bv)
            return out.reshape(b, h, n, d)

        def _layer(x, wqkv, qs, ksc, wo, lg, lb, w1, b1, w2, b2):
            b, n, _ = x.shape
            h = shift_token(x)
            qkv = h @ wqkv
            q, k, v = jnp.split(qkv, 3, axis=-1)
            to_heads = lambda t: t.reshape(b, n, HEADS, DIM_HEAD).transpose(0, 2, 1, 3)
            q, k, v = (to_heads(q), to_heads(k), to_heads(v))
            q = l2norm(q) * qs
            k = l2norm(k) * ksc
            q, k = rotary_xpos(q, k)
            o = local_attention(q, k, v)
            o = o.transpose(0, 2, 1, 3).reshape(b, n, INNER)
            x = x + o @ wo
            h = shift_token(x)
            mu = h.mean(-1, keepdims=True)
            var = h.var(-1, keepdims=True)
            h = (h - mu) / jnp.sqrt(var + 1e-05) * lg + lb
            h = h @ w1 + b1
            a, g = jnp.split(h, 2, axis=-1)
            h = a * jax.nn.gelu(g, approximate=False)
            x = x + h @ w2 + b2
            return x
        for l in range(DEPTH):
            x = _layer(x, wqkv[l], q_scale[l], k_scale[l], wo[l], ln_g[l], ln_b[l], w1[l], b1[l], w2[l], b2[l])
        return x
    x = L0_attn_x
    xn = _layernorm(x, axis=-1)
    x = x + _L0_attn_ref(xn, L0_attn_Wqkv, L0_attn_Wout, L0_attn_head_scales, L0_attn_head_dirs) + _L0_ffn_ref(xn, L0_ffn_wqkv, L0_ffn_q_scale, L0_ffn_k_scale, L0_ffn_wo, L0_ffn_ln_g, L0_ffn_ln_b, L0_ffn_w1, L0_ffn_b1, L0_ffn_w2, L0_ffn_b2)
    return x

_drawn_inputs = setup_inputs


def setup_inputs(seed=0):
    import zlib

    import numpy as np

    out = dict(_drawn_inputs(seed))
    spreads = {'L0_ffn_q_scale': (1.0, 0.6),
     'L0_ffn_k_scale': (1.0, 0.6),
     'L0_ffn_ln_g': (1.0, 0.6),
     'L0_ffn_ln_b': (0.0, 0.8),
     'L0_ffn_b1': (0.0, 0.8),
     'L0_ffn_b2': (0.0, 0.437)}
    factors = {'L0_attn_Wqkv': 8.0,
     'L0_attn_Wout': 8.0,
     'L0_attn_head_scales': 8.0,
     'L0_attn_head_dirs': 8.0,
     'L0_ffn_wqkv': 3.761,
     'L0_ffn_wo': 3.754,
     'L0_ffn_w1': 6.157,
     'L0_ffn_w2': 6.06}
    for name, (base, spread) in spreads.items():
        noise = np.random.default_rng([zlib.crc32(name.encode()), seed]).standard_normal(out[name].shape)
        drawn = base * np.exp(spread * noise) if base else spread * noise
        out[name] = jnp.asarray(drawn.astype(out[name].dtype))
    for name, factor in factors.items():
        out[name] = (out[name] * factor).astype(out[name].dtype)
    return out
```

```python
from contextlib import ExitStack

import numpy as np

import concourse.bass as bass
from concourse import mybir

F32 = mybir.dt.float32
BF16 = mybir.dt.bfloat16
ALU = mybir.AluOpType
ACT = mybir.ActivationFunctionType
AX = mybir.AxisListType

P = 128
B, T, D = 4, 512, 128
NT = T // P
EPS = 1e-5
NEG = -1e30

MH, MD = 8, 16
GH = 4
TERMS = [(0, 0), (0, 1), (0, 2), (1, 0), (1, 1), (2, 0)]
KS = MD * len(TERMS)
KM = KS + 3

DEPTH, FH, FD, WIN = 2, 8, 64, 64
INNER = FH * FD
NP = FH // 2
HID = int(D * 4 * 2 / 3)
CH = [(c, min(P, HID - c)) for c in range(0, HID, P)]
QK_SCALE = 8.0

NB = 2
TURNS = B // NB
GROUPS = [(l, bb) for l in range(DEPTH) for bb in range(NB)]
TILES = [(l, bb, t) for l, bb in GROUPS for t in range(NT)]
NTL = len(TILES)
RING = 7

def max_units(g):
    h = GH * g
    return ([([h + i], 3) for i in range(4)] + [([h + i], 2) for i in range(4)]
            + [([h, h + 1], 1), ([h + 2, h + 3], 1), ([h, h + 1, h + 2, h + 3], 0)])


def exp_units(g):
    h = GH * g
    return ([([h + i], 0) for i in range(4)] + [([h + i], 1) for i in range(4)]
            + [([h, h + 1], 2), ([h + 2, h + 3], 2), ([h, h + 1, h + 2, h + 3], 3)])


NPM = 8
NU = 11
UNITS_OF_J = [range(0, 4), range(4, 8), range(8, 10), range(10, 11)]


FIRST_FILL = 3


def fillers():
    out = []
    for bb in range(NB):
        out += [("mmax", bb, g, k) for g in range(2) for k in range(NU)] + [("mmaxT", bb)]
    for bb in range(NB):
        for g in range(2):
            out += [("mexp", bb, g, k) for k in range(6)] + [("mpv", bb, g, 0)]
            out += [("mexp", bb, g, k) for k in range(6, 10)] + [("mpv", bb, g, 1)]
            out += [("mexp", bb, g, 10), ("mpv", bb, g, 2), ("mpv", bb, g, 3), ("mden", bb, g)]
        out += [("mout", bb)]
    return out


def order():
    out = [("xT", bb) for bb in range(NB)]
    out += [("hT", 0, bb) for bb in range(NB)]
    out += [("mqkv", bb) for bb in range(NB)]
    fill = fillers()
    slots = NTL + 3
    per = -(-len(fill) // (2 * (slots - FIRST_FILL + 1)))
    tail = {}
    for gi in range(len(GROUPS)):
        last = NT * gi + NT - 1
        for at, what in ((last + 2, "wo"), (last + 3, "mean"), (last + 3, "var"), (last + 3, "rstd"),
                         (last + 4, "mlp")):
            tail.setdefault(min(at, slots), []).append((what, gi))
    for s in range(slots + 1):
        if 0 <= s - 1 < NTL:
            out.append(("ropeT", s - 1))
        if s < NTL:
            out.append(("qkv", s))
        if 0 <= s - 2 < NTL:
            out.append(("pv", s - 2))
        late = tail.get(s, [])
        out += [x for x in late if x[0] == "mean"]
        if 0 <= s - 1 < NTL:
            out.append(("smax", s - 1))
        if 0 <= s - 2 < NTL:
            out.append(("oT", s - 2))
        if s >= FIRST_FILL:
            out += fill[:per]
            fill = fill[per:]
        out += [x for x in late if x[0] in ("wo", "var")]
        if 0 <= s - 1 < NTL:
            out.append(("smaxT", s - 1))
        if s >= FIRST_FILL:
            out += fill[:per]
            fill = fill[per:]
        out += [("h2", gi) for what, gi in late if what == "wo"]
        out += [x for x in late if x[0] == "rstd"]
        out += [x for x in late if x[0] == "mlp"]
        if 0 <= s - 1 < NTL:
            out.append(("sexp", s - 1))
        out += [("hT", GROUPS[gi][0] + 1, GROUPS[gi][1]) for what, gi in late
                if what == "mlp" and GROUPS[gi][0] + 1 < DEPTH]
    assert not fill
    out += [("yT", bb) for bb in range(NB)]
    return out


UNITS = {"xT": 1, "mqkv": 3, "qkv": 3, "ropeT": 2, "smax": 2, "smaxT": 1, "sexp": 2, "pv": 2, "oT": 1,
         "wo": 1, "mean": 1, "var": 1, "rstd": 1, "mlp": 2 * len(CH) + 1, "yT": 1, "mmax": 1, "mmaxT": 1,
         "mexp": 1, "mpv": 0, "hT": 0, "h2": 0, "mden": 1, "mout": 1}

IDENT, MEAN, DEN, CAUS, CAUST, WIN1, WINT, WINTE, WIN0, WINT0, COMBO = range(11)
N_CONST = COMBO + 2 * NP


def constants():
    m = np.zeros((N_CONST, P, P), np.float32)
    k, n = np.arange(P)[:, None], np.arange(P)[None, :]
    m[IDENT] = k == n
    m[MEAN] = 1.0 / D
    m[DEN] = k == 32 * (n // 32) + MD
    m[CAUS] = np.where(n <= k, 0.0, NEG)
    m[CAUST] = np.where(n >= k, 0.0, NEG)
    i = k % WIN
    win = np.where(np.where(n < WIN, n >= i, n - WIN <= i), 0.0, NEG)
    m[WIN1] = win
    m[WINT] = win.T
    m[WINTE] = np.roll(win.T, WIN, axis=0)
    m[WIN0] = np.where(n < WIN, NEG, win)
    m[WINT0] = np.where(k >= WIN, NEG, m[WINTE])
    for c in range(2 * NP):
        m[COMBO + c] = (k < 6 * NP) & (k % (2 * NP) == c)
    f = np.float32
    half = np.arange(0, FD, 2).astype(f)
    t = np.arange(T).astype(f)
    freqs = t[:, None] * (f(1.0) / f(10000.0) ** (half / f(FD)))[None, :]
    base = (half + f(0.4 * FD)) / f(1.4 * FD)
    scale = base[None, :] ** ((t - T // 2) / f(WIN // 2))[:, None]
    cos, sin, scale = (np.concatenate([a, a], 1).astype(f) for a in (np.cos(freqs), np.sin(freqs), scale))
    sin[:, :FD // 2] *= -1
    rope = np.stack([cos * scale * f(QK_SCALE), sin * scale * f(QK_SCALE), cos / scale, sin / scale]).astype(f)
    return m, rope


def build(nc, x, Wqkv, Wout, head_scales, head_dirs, wqkv, q_scale, k_scale, wo, ln_g, ln_b, w1, b1, w2, b2,
          consts, rope, out):
    steps = order()
    unit, nth, count = {}, {}, {}
    for st in steps:
        for i in range(UNITS[st[0]]):
            unit[st + (i,)] = len(unit)
            nth[st + (i,)] = count.get(st[0], 0)
            count[st[0]] = nth[st + (i,)] + 1
    by_number = list(unit)

    with ExitStack() as ctx:
        def sb(name, shape, dt=F32):
            return ctx.enter_context(nc.sbuf_tensor(name, shape, dt))

        def sem(name):
            return ctx.enter_context(nc.semaphore(name))

        ps = ctx.enter_context(nc.psum_tensor("ps", [P, RING, 512], F32))
        spill = nc.dram_tensor("spill", (NB, 2, P, 3, T), BF16, kind="Internal").ap()
        acc = ctx.enter_context(nc.psum_tensor("acc", [P, 512], F32))

        cf = sb("cf", [P, CAUS, P])
        cb = sb("cb", [P, N_CONST, P], BF16)
        identf, identb = cf[:, IDENT, :], cb[:, IDENT, :]
        Wm = sb("Wm", [P, 3 * D])
        WoE = sb("WoE", [P, 2, D])
        dirs = sb("dirs", [P, MH, 3])
        hsc = sb("hsc", [P, MH])
        wdot = sb("wdot", [P, MH, 3])
        wgeo = sb("wgeo", [P, 2, MH])
        wgd = sb("wgd", [P, MH, 3])
        Wk2 = sb("Wk2", [P, D])
        Wf = sb("Wf", [P, DEPTH, 3 * INNER])
        Wo = sb("Wo", [P, DEPTH, NP, D])
        W1 = sb("W1", [P, DEPTH, 2 * HID])
        W2 = sb("W2", [P, DEPTH, len(CH), D])
        col = sb("col", [P, DEPTH, 3 + 2 * len(CH)])
        qs = sb("qs", [P, DEPTH, 2, FD])
        rt = sb("rt", [P, DEPTH, 4, NT, FD])

        xtok = sb("xtok", [P, NB, NT, D])
        bst = sb("bst", [P, NB, NT, 6])
        bag = sb("bag", [P, NB, NT, 2])
        vpe = sb("vpe", [P, NB, NT])
        rsx = sb("rsx", [P, NB, NT])
        xT = sb("xT", [P, NB, T])
        hT = sb("hT", [P, NB, T])
        stq = sb("stq", [P, NB, MH, T], BF16)
        stk = sb("stk", [P, NB, MH, T], BF16)
        mv = sb("mv", [P, NB, NT, MH, 32])
        mmx = sb("mmx", [P, NB, NT, MH])
        mmr = sb("mmr", [P, NB, NT * MH])
        mm3 = sb("mm3", [P, NB, P], BF16)
        mmT = sb("mmT", [P, NB, P], BF16)
        pm = sb("pm", [P, NPM, 512])
        oraw = sb("oraw", [P, 2, 512])
        mrec = sb("mrec", [P, 512])
        aT = sb("aT", [P, NB, T])
        sq = sb("sq", [P, 2 * FH, FD])
        ss = sb("ss", [P, 2, 2 * FH])
        ssc = sb("ssc", [P, 2, 2 * FH])
        rn = sb("rn", [P, 2, 2 * FH])
        qkn = sb("qkn", [P, 2, 2 * FH, FD])
        qk = sb("qk", [P, 2 * FH, FD])
        rs = sb("rs", [P, 2 * FH, FD])
        bdq = sb("bdq", [P, 2, NP, 2, 2, WIN])
        kT = sb("kT", [P, NP, WIN + T])
        va = sb("va", [P, NT, FH, FD + 1])
        ve = sb("ve", [P, NT, FH, FD + 1])
        wmx = sb("wmx", [P, 2, 2 * NP])
        wmr = sb("wmr", [P, 2, 2 * NP])
        wm3 = sb("wm3", [P, 2, P], BF16)
        wmT = sb("wmT", [P, 2, P], BF16)
        pw = sb("pw", [P, 2, NP, 2, WIN])
        wrec = sb("wrec", [P, 2, FH])
        otok = sb("otok", [P, 2, FH, FD])
        oT = sb("oT", [P, NP, T])
        hc = sb("hc", [P, T])
        hq = sb("hq", [P, T])
        vl = sb("vl", [P, NT])
        rl = sb("rl", [P, NT])
        mhalf = sb("mhalf", [P, 2 * FH])
        gl = sb("gl", [P, len(CH), T])
        xn = otok[:, :, :, :].rearrange("p b h d -> p (b h d)").rearrange("p (b t d) -> p b t d", b=NB, t=NT)
        yo = xn
        part = pm[:, :, :].rearrange("p k n -> p (k n)")[:, 0:NB * 3 * T].bitcast(BF16)\
            .rearrange("p (b w r n) -> p b w r n", b=NB, w=2, r=3)
        rest = gl
        staged = pm[:, :, :].rearrange("p k n -> p (k n)")[:, 0:(N_CONST - CAUS) * P]\
            .rearrange("p (c n) -> p c n", n=P)
        rp = oT[:, :, :].rearrange("p c n -> p (c n)")[:, 0:4 * NT * FD]\
            .rearrange("p (r t d) -> p r t d", r=4, t=NT)

        NG, NCH = len(GROUPS), len(CH)
        s_wclr = sem("wout_cleared")
        s_load = sem("weights_in")
        s_dset = sem("dve_prologue")
        s_pset = sem("pool_prologue")
        go_pool, go_act, go_dve, go_pe = (sem(f"counts_at_zero_{e}") for e in ("pool", "act", "dve", "pe"))
        s_over = sem("turn_over")
        done = {k: sem("pe_" + k) for k in count}
        s_mpv = sem("pe_mpv")
        s_x = [sem(f"x_in{b}") for b in range(NB)]
        s_st = sem("x_stats")
        s_ag = sem("x_mean_var")
        s_vpe = sem("x_var_eps")
        s_rsx = sem("x_rstd")
        s_xn = sem("x_normed")
        s_xT = sem("xT_ready")
        s_x1 = sem("xT_after_attention")
        s_hT = sem("hT_ready")
        s_hs = sem("hT_for_mlp")
        s_p0 = sem("main_part0")
        s_re = sem("main_rest")
        s_p1 = sem("main_part1")
        s_p2 = sem("main_part2")
        s_spill = [sem(f"main_parts_out{b}") for b in range(NB)]
        s_stk = [sem(f"main_stacks_in{b}") for b in range(NB)]
        s_mv = sem("main_v")
        s_mmx = sem("main_max")
        s_mm = sem("main_max_parts")
        s_mmT = sem("main_max_rows")
        s_mst = [sem(f"main_max_in{b}") for b in range(NB)]
        s_pm = sem("main_exp")
        s_or = sem("main_o_raw")
        s_mrec = sem("main_recip")
        s_on = sem("main_o")
        s_aT = sem("main_result")
        s_sq = sem("win_squares")
        s_ss = sem("win_sumsq")
        s_ssc = sem("win_sumsq_clamped")
        s_rn = sem("win_rnorm")
        s_qkn = sem("win_qk_normed")
        s_rc = sem("rope_cos")
        s_rs = sem("rope_sin")
        s_qk = sem("rope_sum")
        s_va = sem("win_v")
        s_ve = [sem(f"win_v_even_in{t}") for t in range(NT)]
        s_bdq = sem("win_qT")
        s_kT = sem("win_kT")
        s_wmx = sem("win_max")
        s_wm = sem("win_max_parts")
        s_wmT = sem("win_max_rows")
        s_pw = sem("win_exp")
        s_wrec = sem("win_recip")
        s_ot = sem("win_o")
        s_oT = sem("win_oT")
        s_hc = sem("ln_centered")
        s_hq = sem("ln_squares")
        s_vl = sem("ln_var")
        s_rl = sem("ln_rstd")
        s_hu = sem("ln_scaled")
        s_hn = sem("ln_out")
        s_gl = sem("mlp_gelu")
        s_uu = sem("mlp_gated")
        s_y1 = sem("mlp_result")
        s_yT = sem("sum_ready")
        s_yo = sem("rows_ready")
        s_out = [sem(f"stored{b}") for b in range(NB)]
        of_a_turn = range(s_over.num, s_out[-1].num + 1)

        def turn_ends(eng, go):
            eng.drain().then_inc(s_over, 1)
            eng.wait_ge(go, 1)
            eng.sem_clear(go)

        def bank(st, i):
            return ps[:, unit[st + (i,)] % RING, :]

        def last_read(u):
            kind, a, i = u[0], u[1], u[-1]
            if kind == "xT":
                return s_xT, a + 1
            if kind == "mqkv":
                return (s_re, 2 * a + i + 1) if i < 2 else (s_mv, a + 1)
            if kind == "qkv":
                return (s_qkn, 2 * a + i + 1) if i < 2 else (s_va, a + 1)
            if kind == "ropeT":
                return (s_bdq, 2 * a + 2) if i == 0 else (s_kT, a + 1)
            if kind == "smax":
                return s_wmx, 2 * a + i + 1
            if kind == "smaxT":
                return s_wmT, a + 1
            if kind == "sexp":
                return s_pw, 2 * a + i + 1
            if kind == "pv":
                return s_ot, 2 * a + i + 1
            if kind == "oT":
                return s_oT, a + 1
            if kind == "wo":
                return s_x1, a + 1
            if kind == "mean":
                return s_hc, a + 1
            if kind == "var":
                return s_vl, a + 1
            if kind == "rstd":
                return s_hu, a + 1
            if kind == "mlp":
                if i == 2 * NCH:
                    l, bb = GROUPS[a]
                    return (s_xT, NB * (l + 1) + bb + 1) if l + 1 < DEPTH else (s_y1, bb + 1)
                return (s_uu, NCH * a + i // 2 + 1) if i % 2 else (s_gl, NCH * a + i // 2 + 1)
            if kind == "mmax":
                return s_mmx, nth[u] + 1
            if kind == "mmaxT":
                return s_mmT, a + 1
            if kind == "mexp":
                return s_pm, nth[u] + 1
            if kind == "mden":
                return s_mrec, nth[u] + 1
            if kind == "mout":
                return s_aT, a + 1
            assert kind == "yT"
            return s_yo, a + 1

        def emptied(st, i):
            n = unit[st + (i,)]
            return last_read(by_number[n - RING]) if n >= RING else (done[st[0]], 0)

        def filled(st, i):
            return done[st[0]], nth[st + (i,)] + 1

        def tile_of(n):
            l, bb, t = TILES[n]
            return l, bb, t, n // NT

        loads = [
            (Wm[:, :], Wqkv),
            (cf[:, :, :], consts[0:CAUS].rearrange("c p n -> p c n")),
            (staged, consts[CAUS:N_CONST].rearrange("c p n -> p c n")),
            (dirs[:, :, :], head_dirs.rearrange("(a h) d -> a h d", a=1).to_broadcast([P, MH, 3])),
            (hsc[:, :], head_scales.rearrange("(a h) -> a h", a=1).to_broadcast([P, MH])),
            (Wf[:, :, :], wqkv.rearrange("l p n -> p l n")),
            (rp[:, :, :, :], rope.rearrange("r (t p) d -> p r t d", p=P)),
            (Wo[:, :, :, :], wo.rearrange("l (c p) n -> p l c n", p=P)),
            (W1[:, :, :], w1.rearrange("l p n -> p l n")),
        ]
        for l in range(DEPTH):
            for i, a in ((0, q_scale), (1, k_scale)):
                loads.append((qs[:, l, i, :], a[l:l + 1, :].to_broadcast([P, FD])))
            for c, (c0, r) in enumerate(CH):
                loads.append((W2[0:r, l, c, :], w2[l, c0:c0 + r, :]))
                loads.append((col[0:r, l, 3 + c:4 + c], b1[l, c0:c0 + r].rearrange("(p a) -> p a", a=1)))
                loads.append((col[0:r, l, 3 + NCH + c:4 + NCH + c],
                              b1[l, HID + c0:HID + c0 + r].rearrange("(p a) -> p a", a=1)))
            for i, a in ((0, ln_g), (1, ln_b), (2, b2)):
                loads.append((col[:, l, i:i + 1], a[l, :].rearrange("(p a) -> p a", a=1)))
        for h in range(MH):
            g, i = h // GH, h % GH
            loads.append((WoE[32 * i:32 * i + MD, g, :], Wout[MD * h:MD * h + MD, :]))
        N_LOADS = len(loads)
        N_DSET, N_PSET = 8, 10 + 8 * DEPTH
        block = ctx.enter_context(nc.Block())

        @block.sync
        def _(sp):
            sp.wait_ge(s_wclr, 1)
            for dst, src in loads:
                sp.dma_start(dst, src).then_inc(s_load, 16)
            sp.wait_ge(s_pset, 9)
            with sp.Fori(0, TURNS) as turn:
                for bb in range(NB):
                    sp.dma_start(xtok[:, bb, :, :], x[turn * NB + bb].rearrange("(t p) d -> p t d", p=P))\
                        .then_inc(s_x[bb], 16)
                for st in steps:
                    kind = st[0]
                    if kind == "mqkv":
                        bb = st[1]
                        for w in range(2):
                            sp.wait_ge(s_p2, 2 * bb + w + 1)
                            sp.dma_start(spill[bb, w], part[:, bb, w, :, :]).then_inc(s_spill[bb], 16)
                        sp.wait_ge(s_spill[bb], 32)
                        for w, stack in enumerate((stq, stk)):
                            for r, term in enumerate(TERMS):
                                sp.dma_start(
                                    stack[MD * r:MD * r + MD, bb, :, :],
                                    spill[bb, w, :, term[w], :].rearrange("(h d) n -> d h n", h=MH))\
                                    .then_inc(s_stk[bb], 16)
                    elif kind == "mmaxT":
                        bb = st[1]
                        sp.wait_ge(s_mmT, bb + 1)
                        for p in range(3):
                            for i in range(NT):
                                r = NT * MH * p + MH * i
                                sp.dma_start(stq[KS + p:KS + p + 1, bb, :, P * i:P * i + P],
                                                 mmT[r:r + MH, bb, :]).then_inc(s_mst[bb], 16)
                    elif kind == "qkv":
                        n = st[1]
                        l, bb, t, gi = tile_of(n)
                        sp.wait_ge(s_va, n + 1)
                        sp.wait_ge(done["pv"], max(0, 2 * (n - NT + 1)))
                        sp.dma_start(ve[0:WIN, t, :, :], va[0:WIN, t, :, :]).then_inc(s_ve[t], 16)
                        if t + 1 < NT:
                            sp.wait_ge(done["pv"], max(0, 2 * (n - NT + 2)))
                            sp.dma_start(ve[WIN:P, t + 1, :, :], va[WIN:P, t, :, :]).then_inc(s_ve[t + 1], 16)
                    elif kind == "yT":
                        bb = st[1]
                        sp.wait_ge(s_yo, bb + 1)
                        sp.dma_start(out[turn * NB + bb].rearrange("(t p) d -> p t d", p=P),
                                         yo[:, bb, :, :]).then_inc(s_out[bb], 16)
                for bb in range(NB):
                    sp.wait_ge(s_out[bb], 16)
                sp.wait_ge(s_over, 4)
                sp.sem_clear(of_a_turn)
                for go in (go_pool, go_act, go_dve, go_pe):
                    sp.drain().then_inc(go, 1)

        @block.gpsimd
        def _(pool):
            pool.memset(WoE[:, :, :], 0.0).then_inc(s_wclr, 1)
            pool.memset(hT[:, :, :], 0.0).then_inc(s_pset, 1)
            pool.memset(bdq[:, :, :, :, :, :], 0.0).then_inc(s_pset, 1)
            pool.memset(kT[:, :, 0:WIN], 0.0).then_inc(s_pset, 1)
            pool.memset(va[:, :, :, FD:FD + 1], 1.0).then_inc(s_pset, 1)
            pool.memset(ve[:, 0, :, :], 0.0).then_inc(s_pset, 1)
            pool.memset(wm3[:, :, :], 0.0).then_inc(s_pset, 1)
            pool.memset(mhalf[:, :], -0.5).then_inc(s_pset, 1)
            pool.memset(mm3[:, :, :], 0.0).then_inc(s_pset, 1)
            pool.memset(mv[:, :, :, :, MD:32], 1.0).then_inc(s_pset, 1)
            pool.wait_ge(s_pset, 9)
            pool.memset(stk[KS:P, :, :, :], 1.0).then_inc(s_pset, 1)
            pool.wait_ge(s_pset, 10)
            pool.wait_ge(s_load, 16 * N_LOADS)
            for l in range(DEPTH):
                for w in range(2):
                    for j in range(2):
                        for hf in range(2):
                            a = 32 * (hf if j == 0 else 1 - hf)
                            pool.tensor_tensor(
                                rt[:, l, 2 * w + j, :, 32 * hf:32 * hf + 32],
                                rp[:, 2 * w + j, :, 32 * hf:32 * hf + 32],
                                qs[:, l, w:w + 1, a:a + 32].to_broadcast([P, NT, 32]), ALU.mult)\
                                    .then_inc(s_pset, 1)

            pool.wait_ge(s_pset, N_PSET)
            with pool.Fori(0, TURNS) as turn:
                for st in steps:
                    kind = st[0]
                    if kind == "xT" and st[1] == 0:
                        for bb in range(NB):
                            pool.wait_ge(s_vpe, bb + 1)
                            pool.tensor_tensor(rsx[:, bb, :], vpe[:, bb, :], mhalf[:, 0:NT], ALU.pow)\
                                .then_inc(s_rsx, 1)
                    elif kind == "qkv":
                        n = st[1]
                        l, bb, t, gi = tile_of(n)
                        b = n % 2
                        pool.wait_ge(s_ssc, n + 1)
                        pool.tensor_tensor(rn[:, b, :], ssc[:, b, :], mhalf[:, :], ALU.pow).then_inc(s_rn, 1)
                        for w in range(2):
                            pool.wait_ge(s_qkn, 2 * n + w + 1)
                            pool.wait_ge(s_qk, n)
                            hs = slice(FH * w, FH * w + FH)
                            for hf in range(2):
                                lo, hi = 32 * hf, 32 * (1 - hf)
                                pool.tensor_tensor(
                                    rs[:, hs, lo:lo + 32], qkn[:, b, hs, hi:hi + 32],
                                    rt[:, l, 2 * w + 1, t:t + 1, lo:lo + 32].to_broadcast([P, FH, 32]),
                                    ALU.mult).then_inc(s_rs, 1)
                        pool.wait_ge(s_rs, 4 * n + 4)
                        pool.wait_ge(s_rc, 2 * n + 2)
                        pool.tensor_tensor(qk[:, :, :], qk[:, :, :], rs[:, :, :], ALU.add).then_inc(s_qk, 1)
                    elif kind == "rstd":
                        gi = st[1]
                        pool.wait_ge(s_vl, gi + 1)
                        pool.wait_ge(done["rstd"], gi)
                        pool.tensor_tensor(rl[:, :], vl[:, :], mhalf[:, 0:NT], ALU.pow).then_inc(s_rl, 1)
                    elif kind == "mean":
                        gi = st[1]
                        bb = GROUPS[gi][1]
                        pool.wait_ge(s_hc, gi + 1)
                        pool.wait_ge(done["var"], gi)
                        pool.tensor_tensor(hq[:, :], hc[:, :], hc[:, :], ALU.mult).then_inc(s_hq, 1)
                    elif kind == "mden":
                        _, bb, g = st
                        k = 2 * bb + g
                        pool.wait_ge(s_mrec, k + 1)
                        pool.tensor_tensor(oraw[:, g, :], oraw[:, g, :], mrec[:, :], ALU.mult).then_inc(s_on, 1)
                turn_ends(pool, go_pool)

        @block.scalar
        def _(act):
            act.wait_ge(s_load, 16 * N_LOADS)
            act.wait_ge(s_pset, 10)

            def shift(bb, s):
                act.activation(hT[0:64, bb, :], xT[0:64, bb, :], ACT.Copy).then_inc(s, 1)
                act.activation(hT[64:P, bb, 1:T], xT[64:P, bb, 0:T - 1], ACT.Copy).then_inc(s, 1)

            with act.Fori(0, TURNS) as turn:
                for st in steps:
                    kind = st[0]
                    if kind == "hT":
                        l, bb = st[1:]
                        act.wait_ge(s_xT, NB * l + bb + 1)
                        if l:
                            act.wait_ge(s_hc, NB * (l - 1) + bb + 1)
                        shift(bb, s_hT)
                    elif kind == "h2":
                        gi = st[1]
                        bb = GROUPS[gi][1]
                        act.wait_ge(s_x1, gi + 1)
                        act.wait_ge(done["qkv"], 3 * NT * (gi + 1))
                        shift(bb, s_hs)
                    elif kind == "mqkv":
                        bb = st[1]
                        for w in range(2):
                            act.wait_ge(*filled(st, w))
                            src = bank(st, w)
                            act.activation(part[:, bb, w, 0, :], src, ACT.Copy).then_inc(s_p0, 1)
                        act.wait_ge(*filled(st, 2))
                        src = bank(st, 2)
                        act.activation(mv[:, bb, :, :, 0:MD],
                                           src.rearrange("p (t h d) -> p t h d", t=NT, h=MH), ACT.Copy)\
                                               .then_inc(s_mv, 1)
                    elif kind == "ropeT":
                        n = st[1]
                        l, bb, t, gi = tile_of(n)
                        act.wait_ge(*filled(st, 0))
                        src = bank(st, 0).rearrange("p (c w i) -> p c w i", c=NP, w=2)
                        act.wait_ge(done["sexp"], max(0, 2 * (n - 1)))
                        act.activation(bdq[0:64, n % 2, :, :, 0, :], src[0:64], ACT.Copy).then_inc(s_bdq, 1)
                        act.activation(bdq[64:P, n % 2, :, :, 1, :], src[64:P], ACT.Copy).then_inc(s_bdq, 1)
                        act.wait_ge(*filled(st, 1))
                        src = bank(st, 1)
                        act.wait_ge(done["sexp"], max(0, 2 * min(n, NT * gi)))
                        act.activation(kT[:, :, WIN + P * t:WIN + P * (t + 1)],
                                           src.rearrange("p (c i) -> p c i", c=NP), ACT.Copy).then_inc(s_kT, 1)
                    elif kind == "qkv":
                        n = st[1]
                        l, bb, t, gi = tile_of(n)
                        for w in range(2):
                            act.wait_ge(*filled(st, w))
                            src = bank(st, w)
                            act.wait_ge(s_ss, n)
                            act.activation(sq[:, FH * w:FH * w + FH, :],
                                               src.rearrange("p (h d) -> p h d", h=FH), ACT.Square)\
                                                   .then_inc(s_sq, 1)
                        act.wait_ge(*filled(st, 2))
                        src = bank(st, 2)
                        act.wait_ge(done["pv"], max(0, 2 * (n - NT + 1)))
                        act.wait_ge(s_ve[t], 16 * (2 if t else 1) * gi)
                        if t + 1 < NT:
                            act.wait_ge(s_ve[t + 1], 16 * 2 * gi)
                        act.activation(va[:, t, :, 0:FD], src.rearrange("p (h d) -> p h d", h=FH),
                                           ACT.Copy).then_inc(s_va, 1)
                    elif kind == "smaxT":
                        n = st[1]
                        act.wait_ge(*filled(st, 0))
                        src = bank(st, 0)[:, 0:P // 2].bitcast(BF16)
                        act.wait_ge(done["sexp"], max(0, 2 * (n - 1)))
                        act.activation(wmT[:, n % 2, :], src, ACT.Copy).then_inc(s_wmT, 1)
                    elif kind == "sexp":
                        n = st[1]
                        for w in range(2):
                            act.wait_ge(*filled(st, w))
                            src = bank(st, w)
                            act.wait_ge(done["pv"], 2 * n)
                            act.activation(pw[:, w, :, :, :],
                                               src.rearrange("p (c a i) -> p c a i", c=NP, a=2), ACT.Exp)\
                                                   .then_inc(s_pw, 1)
                    elif kind == "oT":
                        n = st[1]
                        l, bb, t, gi = tile_of(n)
                        act.wait_ge(*filled(st, 0))
                        src = bank(st, 0)
                        act.wait_ge(done["wo"], gi)
                        act.activation(oT[:, :, P * t:P * t + P],
                                           src.rearrange("p (c i) -> p c i", c=NP), ACT.Copy).then_inc(s_oT, 1)
                    elif kind == "mlp":
                        gi = st[1]
                        l, bb = GROUPS[gi]
                        for c, (c0, r) in enumerate(CH):
                            act.wait_ge(*filled(st, 2 * c))
                            src = bank(st, 2 * c)
                            act.wait_ge(done["mlp"], (2 * NCH + 1) * gi)
                            k = 3 + NCH + c
                            act.activation(gl[0:r, c, :], src[0:r], ACT.Gelu, bias=col[0:r, l, k:k + 1])\
                                .then_inc(s_gl, 1)
                    elif kind == "mexp":
                        _, bb, g, k = st
                        hs, J = exp_units(g)[k]
                        wd = len(hs) * (T - P * J)
                        act.wait_ge(*filled(st, 0))
                        src = bank(st, 0)
                        act.wait_ge(s_mpv, NT * (2 * bb + g) + (k >= NPM))
                        act.activation(pm[:, k % NPM, 0:wd], src[:, 0:wd], ACT.Exp).then_inc(s_pm, 1)
                    elif kind == "mmaxT":
                        bb = st[1]
                        act.wait_ge(*filled(st, 0))
                        src = bank(st, 0)[:, 0:P // 2].bitcast(BF16)
                        act.activation(mmT[:, bb, :], src, ACT.Copy).then_inc(s_mmT, 1)
                    elif kind == "mout":
                        bb = st[1]
                        act.wait_ge(*filled(st, 0))
                        src = bank(st, 0)
                        act.activation(aT[:, bb, :], src, ACT.Copy).then_inc(s_aT, 1)
                turn_ends(act, go_act)

        @block.vector
        def _(dve):
            dve.wait_ge(s_load, 16 * N_LOADS)
            dve.tensor_copy(cb[:, 0:CAUS, :], cf[:, :, :]).then_inc(s_dset, 1)
            dve.tensor_copy(cb[:, CAUS:N_CONST, :], staged).then_inc(s_dset, 1)
            wk = Wm[:, D:2 * D].rearrange("p (h d) -> p h d", h=MH)
            wk2 = Wk2[:, :].rearrange("p (h d) -> p h d", h=MH)
            dve.tensor_tensor(wdot[:, :, :], wk[:, :, 0:3], dirs[:, :, :], ALU.mult).then_inc(s_dset, 1)
            dve.wait_ge(s_dset, 3)
            dve.tensor_reduce(wgeo[:, 0, :], wdot[:, :, :], AX.X, ALU.add).then_inc(s_dset, 1)
            dve.wait_ge(s_dset, 4)
            dve.tensor_tensor(wgeo[:, 1, :], wgeo[:, 0, :], hsc[:, :], ALU.mult).then_inc(s_dset, 1)
            dve.wait_ge(s_dset, 5)
            dve.tensor_tensor(wgd[:, :, :], dirs[:, :, :],
                                  wgeo[:, 1, :].rearrange("p (h a) -> p h a", a=1).to_broadcast([P, MH, 3]),
                                  ALU.mult).then_inc(s_dset, 1)
            dve.tensor_scalar(Wk2[:, :], Wm[:, D:2 * D], float(MD) ** -0.5, None, ALU.mult).then_inc(s_dset, 1)
            dve.wait_ge(s_dset, 7)
            dve.tensor_tensor(wk2[:, :, 0:3], wk2[:, :, 0:3], wgd[:, :, :], ALU.add).then_inc(s_dset, 1)
            dve.wait_ge(s_pset, N_PSET)

            def split(src, p0, rest_, p1, p2, s, n):
                dve.tensor_copy(p0, src).then_inc(s, 1)
                dve.wait_ge(s, n + 1)
                dve.tensor_tensor(rest_, src, p0, ALU.subtract).then_inc(s, 1)
                dve.wait_ge(s, n + 2)
                dve.tensor_copy(p1, rest_).then_inc(s, 1)
                dve.wait_ge(s, n + 3)
                dve.tensor_tensor(p2, rest_, p1, ALU.subtract).then_inc(s, 1)

            with dve.Fori(0, TURNS) as turn:
                for st in steps:
                    kind = st[0]
                    if kind == "xT":
                        bb = st[1]
                        if bb == 0:
                            for c in range(NB):
                                dve.wait_ge(s_x[c], 16)
                                for t in range(NT):
                                    dve.bn_stats(bst[:, c, t, :], xtok[:, c, t, :]).then_inc(s_st, 1)
                                dve.wait_ge(s_st, NT * (c + 1))
                                for t in range(NT):
                                    dve.bn_aggr(bag[:, c, t, :], bst[:, c, t, :]).then_inc(s_ag, 1)
                                dve.wait_ge(s_ag, NT * (c + 1))
                                dve.tensor_scalar(vpe[:, c, :], bag[:, c, :, 1], EPS, None, ALU.add)\
                                    .then_inc(s_vpe, 1)
                            for c in range(NB):
                                dve.wait_ge(s_rsx, c + 1)
                                for t in range(NT):
                                    dve.tensor_scalar(xn[:, c, t, :], xtok[:, c, t, :], bag[:, c, t, 0:1],
                                                          rsx[:, c, t:t + 1], ALU.subtract, ALU.mult)\
                                                              .then_inc(s_xn, 1)
                        dve.wait_ge(*filled(st, 0))
                        src = bank(st, 0)
                        dve.tensor_copy(xT[:, bb, :], src).then_inc(s_xT, 1)
                    elif kind == "mqkv":
                        bb = st[1]
                        for w in range(2):
                            i = 2 * bb + w
                            dve.wait_ge(*filled(st, w))
                            src = bank(st, w)
                            dve.wait_ge(s_p0, i + 1)
                            dve.wait_ge(s_p2, max(0, i - 1))
                            dve.tensor_tensor(rest[:, w, :], src, part[:, bb, w, 0, :], ALU.subtract)\
                                .then_inc(s_re, 1)
                            dve.wait_ge(s_re, i + 1)
                            dve.tensor_copy(part[:, bb, w, 1, :], rest[:, w, :]).then_inc(s_p1, 1)
                            dve.wait_ge(s_p1, i + 1)
                            dve.tensor_tensor(part[:, bb, w, 2, :], rest[:, w, :], part[:, bb, w, 1, :],
                                                  ALU.subtract).then_inc(s_p2, 1)
                    elif kind == "qkv":
                        n = st[1]
                        l, bb, t, gi = tile_of(n)
                        b = n % 2
                        dve.wait_ge(s_sq, 2 * n + 2)
                        dve.tensor_reduce(ss[:, b, :], sq[:, :, :], AX.X, ALU.add).then_inc(s_ss, 1)
                        dve.wait_ge(s_ss, n + 1)
                        dve.tensor_scalar(ssc[:, b, :], ss[:, b, :], 1e-24, None, ALU.max).then_inc(s_ssc, 1)
                        for w in range(2):
                            hs = slice(FH * w, FH * w + FH)
                            dve.wait_ge(*filled(st, w))
                            src = bank(st, w).rearrange("p (h d) -> p h d", h=FH)
                            dve.wait_ge(s_rn, n + 1)
                            dve.wait_ge(s_rs, max(0, 4 * (n - 1)))
                            dve.tensor_tensor(
                                qkn[:, b, hs, :], src,
                                rn[:, b, hs].rearrange("p (h a) -> p h a", a=1).to_broadcast([P, FH, FD]),
                                ALU.mult).then_inc(s_qkn, 1)
                        for w in range(2):
                            hs = slice(FH * w, FH * w + FH)
                            dve.wait_ge(s_qkn, 2 * n + w + 1)
                            dve.wait_ge(done["ropeT"], 2 * n)
                            dve.tensor_tensor(
                                qk[:, hs, :], qkn[:, b, hs, :],
                                rt[:, l, 2 * w, t:t + 1, :].to_broadcast([P, FH, FD]), ALU.mult)\
                                    .then_inc(s_rc, 1)
                    elif kind == "smax":
                        n = st[1]
                        b = n % 2
                        for w in range(2):
                            dve.wait_ge(*filled(st, w))
                            src = bank(st, w).rearrange("p (c j) -> p c j", c=NP)
                            dve.wait_ge(s_wm, max(0, 4 * (n - 1)))
                            dve.tensor_reduce(wmx[:, b, NP * w:NP * w + NP], src, AX.X, ALU.max,
                                                  negate=True).then_inc(s_wmx, 1)
                        dve.wait_ge(s_wmx, 2 * n + 2)
                        dve.wait_ge(done["smaxT"], max(0, n - 1))
                        k = 2 * NP
                        split(wmx[:, b, :], wm3[:, b, 0:k], wmr[:, b, :], wm3[:, b, k:2 * k],
                              wm3[:, b, 2 * k:3 * k], s_wm, 4 * n)
                    elif kind == "pv":
                        n = st[1]
                        b = n % 2
                        for i in range(2):
                            dve.wait_ge(*filled(st, i))
                            src = bank(st, i)[:, 0:4 * (FD + 1)].rearrange("p (h d) -> p h d", h=4)
                            hs = slice(4 * i, 4 * i + 4)
                            dve.wait_ge(s_ot, max(0, 2 * (n - 2) + i + 1))
                            dve.reciprocal(wrec[:, b, hs], src[:, :, FD]).then_inc(s_wrec, 1)
                            dve.wait_ge(s_wrec, 2 * n + i + 1)
                            dve.wait_ge(done["oT"], max(0, n - 1))
                            dve.tensor_tensor(
                                otok[:, b, hs, :], src[:, :, 0:FD],
                                wrec[:, b, hs].rearrange("p (h a) -> p h a", a=1).to_broadcast([P, 4, FD]),
                                ALU.mult).then_inc(s_ot, 1)
                    elif kind == "wo":
                        gi = st[1]
                        l, bb = GROUPS[gi]
                        dve.wait_ge(*filled(st, 0))
                        src = bank(st, 0)
                        dve.wait_ge(s_hT, 2 * (NB * l + bb) + 2)
                        dve.wait_ge(done["mqkv"], 3 * NB)
                        dve.tensor_tensor(xT[:, bb, :], src, xT[:, bb, :], ALU.add).then_inc(s_x1, 1)
                    elif kind == "mean":
                        gi = st[1]
                        bb = GROUPS[gi][1]
                        dve.wait_ge(*filled(st, 0))
                        src = bank(st, 0)
                        dve.wait_ge(done["mlp"], (2 * NCH + 1) * gi)
                        dve.tensor_tensor(hc[:, :], hT[:, bb, :], src, ALU.subtract).then_inc(s_hc, 1)
                    elif kind == "var":
                        gi = st[1]
                        dve.wait_ge(*filled(st, 0))
                        src = bank(st, 0)
                        dve.wait_ge(s_rl, gi)
                        dve.tensor_scalar(vl[:, :], src[:, 0:NT], EPS, None, ALU.add).then_inc(s_vl, 1)
                    elif kind == "rstd":
                        gi = st[1]
                        l, bb = GROUPS[gi]
                        dve.wait_ge(*filled(st, 0))
                        src = bank(st, 0)
                        dve.wait_ge(s_hq, gi + 1)
                        dve.tensor_tensor(hc[:, :], hc[:, :], src, ALU.mult).then_inc(s_hu, 1)
                        dve.wait_ge(s_hu, gi + 1)
                        dve.tensor_scalar(hc[:, :], hc[:, :], col[:, l, 0:1], col[:, l, 1:2],
                                          ALU.mult, ALU.add).then_inc(s_hn, 1)
                    elif kind == "mlp":
                        gi = st[1]
                        l, bb = GROUPS[gi]
                        for c, (c0, r) in enumerate(CH):
                            dve.wait_ge(*filled(st, 2 * c + 1))
                            src = bank(st, 2 * c + 1)
                            dve.wait_ge(s_gl, NCH * gi + c + 1)
                            dve.scalar_tensor_tensor(out=gl[0:r, c, :], in0=src[0:r],
                                                         scalar=col[0:r, l, 3 + c:4 + c], in1=gl[0:r, c, :],
                                                         op0=ALU.add, op1=ALU.mult).then_inc(s_uu, 1)
                        dve.wait_ge(*filled(st, 2 * NCH))
                        src = bank(st, 2 * NCH)
                        dve.wait_ge(s_hs, 2 * gi + 2)
                        dve.scalar_tensor_tensor(out=xT[:, bb, :], in0=src, scalar=col[:, l, 2:3],
                                                     in1=xT[:, bb, :], op0=ALU.add, op1=ALU.add)\
                                                         .then_inc(s_xT if l + 1 < DEPTH else s_y1, 1)
                    elif kind == "mmax":
                        _, bb, g, k = st
                        hs, I = max_units(g)[k]
                        wd = P * (I + 1)
                        dve.wait_ge(*filled(st, 0))
                        src = bank(st, 0)[:, 0:len(hs) * wd].rearrange("p (h j) -> p h j", j=wd)
                        dve.tensor_reduce(mmx[:, bb, I, hs[0]:hs[-1] + 1], src, AX.X, ALU.max,
                                              negate=True).then_inc(s_mmx, 1)
                    elif kind == "mmaxT":
                        bb = st[1]
                        dve.wait_ge(s_mmx, 2 * NU * (bb + 1))
                        k = NT * MH
                        split(mmx[:, bb, :, :].rearrange("p i h -> p (i h)"), mm3[:, bb, 0:k],
                              mmr[:, bb, :], mm3[:, bb, k:2 * k], mm3[:, bb, 2 * k:3 * k], s_mm, 4 * bb)
                    elif kind == "mden":
                        _, bb, g = st
                        k = 2 * bb + g
                        dve.wait_ge(s_mpv, NT * (k + 1))
                        dve.wait_ge(s_on, k)
                        dve.wait_ge(done["mout"], bb)
                        dve.tensor_copy(oraw[:, g, :], acc[:, :]).then_inc(s_or, 1)
                        dve.wait_ge(*filled(st, 0))
                        src = bank(st, 0)
                        dve.reciprocal(mrec[:, :], src).then_inc(s_mrec, 1)
                    elif kind == "yT":
                        bb = st[1]
                        dve.wait_ge(s_aT, bb + 1)
                        dve.wait_ge(s_y1, bb + 1)
                        dve.tensor_tensor(aT[:, bb, :], xT[:, bb, :], aT[:, bb, :], ALU.add).then_inc(s_yT, 1)
                        dve.wait_ge(*filled(st, 0))
                        src = bank(st, 0)
                        dve.tensor_tensor(yo[:, bb, :, :].rearrange("p t d -> p (t d)"), src,
                                              xtok[:, bb, :, :].rearrange("p t d -> p (t d)"), ALU.add)\
                                                  .then_inc(s_yo, 1)
                turn_ends(dve, go_dve)

        @block.tensor
        def _(pe):
            pe.wait_ge(s_load, 16 * N_LOADS)
            pe.wait_ge(s_dset, N_DSET)
            pe.wait_ge(s_pset, N_PSET)

            def mm(o, a, b, start=True, stop=True):
                return pe.matmul(o, a, b, start=start, stop=stop)

            with pe.Fori(0, TURNS) as turn:
                for st in steps:
                    kind = st[0]
                    if kind == "xT":
                        bb = st[1]
                        pe.wait_ge(*emptied(st, 0))
                        o = bank(st, 0)
                        pe.wait_ge(s_xn, NT * (bb + 1))
                        for t in range(NT):
                            i = pe.transpose(o[:, P * t:P * t + P], xn[:, bb, t, :], identf)
                        i.then_inc(done[kind], 1)
                    elif kind == "mqkv":
                        bb = st[1]
                        pe.wait_ge(s_xT, bb + 1)
                        pe.wait_ge(*emptied(st, 0))
                        mm(bank(st, 0), Wm[:, 0:D], xT[:, bb, :]).then_inc(done[kind], 1)
                        pe.wait_ge(*emptied(st, 1))
                        mm(bank(st, 1), Wk2[:, :], xT[:, bb, :]).then_inc(done[kind], 1)
                        pe.wait_ge(*emptied(st, 2))
                        o = bank(st, 2)
                        for t in range(NT):
                            i = mm(o[:, P * t:P * t + P], xT[:, bb, P * t:P * t + P], Wm[:, 2 * D:3 * D])
                        i.then_inc(done[kind], 1)
                    elif kind == "qkv":
                        n = st[1]
                        l, bb, t, gi = tile_of(n)
                        pe.wait_ge(s_hT, 2 * (NB * l + bb) + 2)
                        for w in range(3):
                            pe.wait_ge(*emptied(st, w))
                            o = bank(st, w)
                            mm(o, hT[:, bb, P * t:P * t + P], Wf[:, l, INNER * w:INNER * (w + 1)])\
                                .then_inc(done[kind], 1)
                    elif kind == "ropeT":
                        n = st[1]
                        pe.wait_ge(s_qk, n + 1)
                        for w in range(2):
                            pe.wait_ge(*emptied(st, w))
                            o = bank(st, w)
                            for c in range(NP):
                                h = FH * w + 2 * c
                                i = pe.transpose(o[:, P * c:P * c + P],
                                                 qk[:, h:h + 2, :].rearrange("p h d -> p (h d)"), identf)
                            i.then_inc(done[kind], 1)
                    elif kind == "smax":
                        n = st[1]
                        l, bb, t, gi = tile_of(n)
                        pe.wait_ge(s_bdq, 2 * n + 2)
                        pe.wait_ge(s_kT, n + 1)
                        for w in range(2):
                            pe.wait_ge(*emptied(st, w))
                            o = bank(st, w)
                            m = WIN0 if t == 0 and w == 0 else WIN1
                            mm(o, identb, cb[:, m:m + 1, :].to_broadcast([P, NP, P]), True, False)
                            for c in range(NP):
                                k0 = P * t + WIN * w
                                i = mm(o[:, P * c:P * c + P],
                                       bdq[:, n % 2, c, w, :, :].rearrange("p a i -> p (a i)"),
                                       kT[:, c, k0:k0 + P], False, c == NP - 1)
                            i.then_inc(done[kind], 1)
                    elif kind == "smaxT":
                        n = st[1]
                        pe.wait_ge(*emptied(st, 0))
                        o = bank(st, 0)
                        pe.wait_ge(s_wm, 4 * n + 4)
                        pe.transpose(o[:, 0:P // 2].bitcast(BF16), wm3[:, n % 2, :], identb)\
                            .then_inc(done[kind], 1)
                    elif kind == "sexp":
                        n = st[1]
                        l, bb, t, gi = tile_of(n)
                        pe.wait_ge(s_wmT, n + 1)
                        for w in range(2):
                            pe.wait_ge(*emptied(st, w))
                            o = bank(st, w)
                            m = WINT if w else (WINT0 if t == 0 else WINTE)
                            mm(o, identb, cb[:, m:m + 1, :].to_broadcast([P, NP, P]), True, False)
                            for c in range(NP):
                                k0 = P * t + WIN * w
                                q = bdq[:, n % 2, c, w, :, :].rearrange("p a i -> p (a i)")
                                oc = o[:, P * c:P * c + P]
                                if w:
                                    mm(oc, kT[:, c, k0:k0 + P], q, False, False)
                                else:
                                    mm(oc[0:WIN], kT[:, c, k0 + WIN:k0 + P], q, False, False)
                                    mm(oc[WIN:P], kT[:, c, k0:k0 + WIN], q, False, False)
                            for c in range(NP):
                                i = mm(o[:, P * c:P * c + P], cb[:, COMBO + NP * w + c, :], wmT[:, n % 2, :],
                                       False, c == NP - 1)
                            i.then_inc(done[kind], 1)
                    elif kind == "pv":
                        n = st[1]
                        l, bb, t, gi = tile_of(n)
                        pe.wait_ge(s_pw, 2 * n + 2)
                        pe.wait_ge(s_va, n + 1)
                        pe.wait_ge(s_ve[t], 16 * (2 if t else 1) * (gi + 1))
                        for u in range(2):
                            pe.wait_ge(*emptied(st, u))
                            o = bank(st, u)
                            for k in range(4):
                                h = 4 * u + k
                                for w, v in ((0, ve), (1, va)):
                                    i = mm(o[WIN * w:WIN * w + WIN, (FD + 1) * k:(FD + 1) * (k + 1)],
                                           pw[:, w, h // 2, h % 2, :], v[:, t, h, :])
                            i.then_inc(done[kind], 1)
                    elif kind == "oT":
                        n = st[1]
                        pe.wait_ge(*emptied(st, 0))
                        o = bank(st, 0)
                        pe.wait_ge(s_ot, 2 * n + 2)
                        for c in range(NP):
                            i = pe.transpose(o[:, P * c:P * c + P],
                                             otok[:, n % 2, 2 * c:2 * c + 2, :].rearrange("p h d -> p (h d)"),
                                             identf)
                        i.then_inc(done[kind], 1)
                    elif kind == "wo":
                        gi = st[1]
                        l, bb = GROUPS[gi]
                        pe.wait_ge(*emptied(st, 0))
                        o = bank(st, 0)
                        pe.wait_ge(s_oT, NT * (gi + 1))
                        for c in range(NP):
                            i = mm(o, Wo[:, l, c, :], oT[:, c, :], c == 0, c == NP - 1)
                        i.then_inc(done[kind], 1)
                    elif kind == "mean":
                        gi = st[1]
                        bb = GROUPS[gi][1]
                        pe.wait_ge(*emptied(st, 0))
                        o = bank(st, 0)
                        pe.wait_ge(s_hs, 2 * gi + 2)
                        mm(o, cf[:, MEAN, :], hT[:, bb, :]).then_inc(done[kind], 1)
                    elif kind == "var":
                        gi = st[1]
                        pe.wait_ge(*emptied(st, 0))
                        o = bank(st, 0)
                        pe.wait_ge(s_hq, gi + 1)
                        for t in range(NT):
                            i = mm(o[:, t:t + 1], hq[:, P * t:P * t + P], cf[:, MEAN, 0:1])
                        i.then_inc(done[kind], 1)
                    elif kind == "rstd":
                        gi = st[1]
                        pe.wait_ge(*emptied(st, 0))
                        o = bank(st, 0)
                        pe.wait_ge(s_rl, gi + 1)
                        for t in range(NT):
                            i = mm(o[:, P * t:P * t + P], rl[:, t:t + 1].to_broadcast([P, P]), identf)
                        i.then_inc(done[kind], 1)
                    elif kind == "mlp":
                        gi = st[1]
                        l, bb = GROUPS[gi]
                        pe.wait_ge(s_hn, gi + 1)
                        for c, (c0, r) in enumerate(CH):
                            for i, first in ((0, HID + c0), (1, c0)):
                                pe.wait_ge(*emptied(st, 2 * c + i))
                                o = bank(st, 2 * c + i)
                                mm(o[0:r], W1[:, l, first:first + r], hc[:, :]).then_inc(done[kind], 1)
                        pe.wait_ge(*emptied(st, 2 * NCH))
                        o = bank(st, 2 * NCH)
                        for c, (c0, r) in enumerate(CH):
                            pe.wait_ge(s_uu, NCH * gi + c + 1)
                            i = mm(o, W2[0:r, l, c, :], gl[0:r, c, :], c == 0, c == NCH - 1)
                        i.then_inc(done[kind], 1)
                    elif kind == "mmax":
                        _, bb, g, k = st
                        hs, I = max_units(g)[k]
                        wd = P * (I + 1)
                        pe.wait_ge(*emptied(st, 0))
                        o = bank(st, 0)
                        pe.wait_ge(s_stk[bb], 16 * 2 * len(TERMS))
                        for j, h in enumerate(hs):
                            mm(o[:, wd * j:wd * (j + 1)], stq[0:KS, bb, h, P * I:P * I + P],
                               stk[0:KS, bb, h, 0:wd], True, False)
                            i = mm(o[:, wd * j + P * I:wd * (j + 1)], identb, cb[:, CAUS, :], False, True)
                        i.then_inc(done[kind], 1)
                    elif kind == "mmaxT":
                        bb = st[1]
                        pe.wait_ge(*emptied(st, 0))
                        o = bank(st, 0)
                        pe.wait_ge(s_mm, 4 * bb + 4)
                        pe.transpose(o[:, 0:P // 2].bitcast(BF16), mm3[:, bb, :], identb)\
                            .then_inc(done[kind], 1)
                    elif kind == "mexp":
                        _, bb, g, k = st
                        hs, J = exp_units(g)[k]
                        wd = T - P * J
                        pe.wait_ge(*emptied(st, 0))
                        o = bank(st, 0)
                        pe.wait_ge(s_mst[bb], 16 * 3 * NT)
                        for j, h in enumerate(hs):
                            mm(o[:, wd * j:wd * (j + 1)], stk[0:KM, bb, h, P * J:P * J + P],
                               stq[0:KM, bb, h, P * J:T], True, False)
                            i = mm(o[:, wd * j:wd * j + P], identb, cb[:, CAUST, :], False, True)
                        i.then_inc(done[kind], 1)
                    elif kind == "mpv":
                        _, bb, g, J = st
                        wd = T - P * J
                        n = 2 * bb + g
                        pe.wait_ge(s_mv, bb + 1)
                        if J == 0:
                            pe.wait_ge(s_or, n)
                        for k in UNITS_OF_J[J]:
                            pe.wait_ge(s_pm, NU * n + k + 1)
                        for k in UNITS_OF_J[J]:
                            for j, h in enumerate(exp_units(g)[k][0]):
                                p0 = 32 * (h % GH)
                                i = mm(acc[p0:p0 + 32, P * J:T], mv[:, bb, J, h, :],
                                       pm[:, k % NPM, wd * j:wd * (j + 1)], J == 0, J == NT - 1)
                        i.then_inc(s_mpv, 1)
                    elif kind == "mden":
                        _, bb, g = st
                        pe.wait_ge(*emptied(st, 0))
                        o = bank(st, 0)
                        pe.wait_ge(s_or, 2 * bb + g + 1)
                        mm(o, cf[:, DEN, :], oraw[:, g, :]).then_inc(done[kind], 1)
                    elif kind == "mout":
                        bb = st[1]
                        pe.wait_ge(*emptied(st, 0))
                        o = bank(st, 0)
                        pe.wait_ge(s_on, 2 * bb + 2)
                        for g in range(2):
                            i = mm(o, WoE[:, g, :], oraw[:, g, :], g == 0, g == 1)
                        i.then_inc(done[kind], 1)
                    elif kind == "yT":
                        bb = st[1]
                        pe.wait_ge(*emptied(st, 0))
                        o = bank(st, 0)
                        pe.wait_ge(s_yT, bb + 1)
                        for t in range(NT):
                            i = pe.transpose(o[:, P * t:P * t + P], aT[:, bb, P * t:P * t + P], identf)
                        i.then_inc(done[kind], 1)
                turn_ends(pe, go_pe)


_INS = ["L0_attn_x", "L0_attn_Wqkv", "L0_attn_Wout", "L0_attn_head_scales", "L0_attn_head_dirs", "L0_ffn_wqkv",
        "L0_ffn_q_scale", "L0_ffn_k_scale", "L0_ffn_wo", "L0_ffn_ln_g", "L0_ffn_ln_b", "L0_ffn_w1", "L0_ffn_b1",
        "L0_ffn_w2", "L0_ffn_b2"]


def kernel(**inputs):
    import numpy as _np
    import concourse.bacc as _bacc
    from concourse import mybir as _mybir
    from concourse.bass_utils import run_bass_kernel_spmd as _run

    nc = _bacc.Bacc("TRN2", target_bir_lowering=False, num_devices=1)
    arrays, args = {}, []
    given = [(n, _np.ascontiguousarray(inputs[n])) for n in _INS] + list(zip(("consts", "rope"), constants()))
    for name, a in given:
        arrays[f"in_{name}_dram"] = a
        args.append(nc.dram_tensor(f"in_{name}_dram", a.shape, _mybir.dt.from_np(a.dtype),
                                   kind="ExternalInput").ap())
    args.append(nc.dram_tensor("out_0_dram", (B, T, D), _mybir.dt.float32, kind="ExternalOutput").ap())
    build(nc, *args)
    r = _run(nc, [arrays], core_ids=[0])
    return r.results[0]["out_0_dram"]
```

```python
from contextlib import ExitStack

import numpy as np

import concourse.bass as bass
from concourse import mybir

F32 = mybir.dt.float32
BF16 = mybir.dt.bfloat16
ALU = mybir.AluOpType
ACT = mybir.ActivationFunctionType
AX = mybir.AxisListType

P = 128
B, T, D = 4, 512, 128
NT = T // P
EPS = 1e-5
NEG = -1e30

MH, MD = 8, 16
GH = 4
TERMS = [(0, 0), (0, 1), (0, 2), (1, 0), (1, 1), (2, 0)]
KS = MD * len(TERMS)
KM = KS + 3

DEPTH, FH, FD, WIN = 2, 8, 64, 64
INNER = FH * FD
NP = FH // 2
HID = int(D * 4 * 2 / 3)
CH = [(c, min(P, HID - c)) for c in range(0, HID, P)]
QK_SCALE = 8.0

NB = 2
TURNS = B // NB
GROUPS = [(l, bb) for l in range(DEPTH) for bb in range(NB)]
TILES = [(l, bb, t) for l, bb in GROUPS for t in range(NT)]
NTL = len(TILES)
HELD, RING = 2, 5

def max_units(g):
    h = GH * g
    return ([([h + i], 3) for i in range(4)] + [([h + i], 2) for i in range(4)]
            + [([h, h + 1], 1), ([h + 2, h + 3], 1), ([h, h + 1, h + 2, h + 3], 0)])


def exp_units(g):
    h = GH * g
    return ([([h + i], 0) for i in range(4)] + [([h + i], 1) for i in range(4)]
            + [([h, h + 1], 2), ([h + 2, h + 3], 2), ([h, h + 1, h + 2, h + 3], 3)])


NPM = 8
NU = 11
UNITS_OF_J = [range(0, 4), range(4, 8), range(8, 10), range(10, 11)]


FIRST_FILL = 3


def fillers():
    out = []
    for bb in range(NB):
        out += [("mmax", bb, g, k) for g in range(2) for k in range(NU)] + [("mmaxT", bb)]
    for bb in range(NB):
        for g in range(2):
            out += [("mexp", bb, g, k) for k in range(6)] + [("mpv", bb, g, 0)]
            out += [("mexp", bb, g, k) for k in range(6, 10)] + [("mpv", bb, g, 1)]
            out += [("mexp", bb, g, 10), ("mpv", bb, g, 2), ("mpv", bb, g, 3), ("mden", bb, g)]
        out += [("mout", bb)]
    return out


def order():
    out = [("xT", bb) for bb in range(NB)]
    out += [("hT", 0, bb) for bb in range(NB)]
    out += [("mqkv", bb) for bb in range(NB)]
    fill = fillers()
    slots = NTL + 2
    per = -(-len(fill) // (2 * (slots - FIRST_FILL + 1)))
    tail = {}
    for gi in range(len(GROUPS)):
        last = NT * gi + NT - 1
        for at, what in ((last + 2, "wo"), (last + 3, "mean"), (last + 3, "var"), (last + 3, "rstd"),
                         (last + 4, "mlp")):
            tail.setdefault(min(at, slots), []).append((what, gi))
    for s in range(slots + 1):
        late = tail.get(s, [])
        if s < NTL:
            out.append(("qkv", s))
        if 0 <= s - 1 < NTL:
            out.append(("ropeT", s - 1))
        if s < NTL:
            out.append(("sums", s))
        if 0 <= s - 2 < NTL:
            out.append(("pv", s - 2))
        out += [x for x in late if x[0] == "mean"]
        if s >= FIRST_FILL:
            out += fill[:per]
            fill = fill[per:]
        if 0 <= s - 1 < NTL:
            out += [("score", s - 1), ("exp", s - 1)]
        if s < NTL:
            out.append(("norm", s))
        out += [x for x in late if x[0] in ("wo", "var")]
        if s >= FIRST_FILL:
            out += fill[:per]
            fill = fill[per:]
        if 0 <= s - 1 < NTL:
            out.append(("weights", s - 1))
        out += [("h2", gi) for what, gi in late if what == "wo"]
        if s < NTL:
            out.append(("rope", s))
        out += [x for x in late if x[0] == "rstd"]
        if 0 <= s - 1 < NTL:
            out.append(("wT", s - 1))
        out += [x for x in late if x[0] == "mlp"]
        out += [("hT", GROUPS[gi][0] + 1, GROUPS[gi][1]) for what, gi in late
                if what == "mlp" and GROUPS[gi][0] + 1 < DEPTH]
    assert not fill
    out += [("yT", bb) for bb in range(NB)]
    return out


UNITS = {"xT": 1, "mqkv": 3, "qkv": 3, "ropeT": 2, "score": 2, "wT": 2, "pv": 1,
         "wo": 1, "mean": 1, "var": 1, "rstd": 1, "mlp": 2 * len(CH) + 1, "yT": 1, "mmax": 1, "mmaxT": 1,
         "mexp": 1, "mpv": 0, "hT": 0, "h2": 0, "sums": 0, "norm": 0, "rope": 0, "exp": 0, "weights": 0,
         "mden": 1, "mout": 1}

IDENT, MEAN, DEN, CAUS, CAUST, WIN1, WINE, WIN0 = range(8)
N_CONST = WIN0 + 1


def constants():
    m = np.zeros((N_CONST, P, P), np.float32)
    k, n = np.arange(P)[:, None], np.arange(P)[None, :]
    m[IDENT] = k == n
    m[MEAN] = 1.0 / D
    m[DEN] = k == 32 * (n // 32) + MD
    m[CAUS] = np.where(n <= k, 0.0, NEG)
    m[CAUST] = np.where(n >= k, 0.0, NEG)
    i = k % WIN
    win = np.where(np.where(n < WIN, n >= i, n - WIN <= i), 0.0, NEG)
    m[WIN1] = win
    m[WINE] = np.roll(win, WIN, axis=1)
    m[WIN0] = np.where(n < WIN, m[WINE], NEG)
    f = np.float32
    half = np.arange(0, FD, 2).astype(f)
    t = np.arange(T).astype(f)
    freqs = t[:, None] * (f(1.0) / f(10000.0) ** (half / f(FD)))[None, :]
    base = (half + f(0.4 * FD)) / f(1.4 * FD)
    scale = base[None, :] ** ((t - T // 2) / f(WIN // 2))[:, None]
    cos, sin, scale = (np.concatenate([a, a], 1).astype(f) for a in (np.cos(freqs), np.sin(freqs), scale))
    sin[:, :FD // 2] *= -1
    rope = np.stack([cos * scale * f(QK_SCALE), sin * scale * f(QK_SCALE), cos / scale, sin / scale]).astype(f)
    return m, rope


def build(nc, x, Wqkv, Wout, head_scales, head_dirs, wqkv, q_scale, k_scale, wo, ln_g, ln_b, w1, b1, w2, b2,
          consts, rope, out):
    steps = order()
    bank_of, before, nth, count, held, ring = {}, {}, {}, {}, [], []
    for st in steps:
        for i in range(UNITS[st[0]]):
            u = st + (i,)
            nth[u] = count.get(st[0], 0)
            count[st[0]] = nth[u] + 1
            turns, first, size = (held, 0, HELD) if st[0] == "qkv" and i < 2 else (ring, HELD, RING)
            bank_of[u] = first + len(turns) % size
            before[u] = turns[-size] if len(turns) >= size else None
            turns.append(u)

    with ExitStack() as ctx:
        def sb(name, shape, dt=F32):
            return ctx.enter_context(nc.sbuf_tensor(name, shape, dt))

        def sem(name):
            return ctx.enter_context(nc.semaphore(name))

        ps = ctx.enter_context(nc.psum_tensor("ps", [P, HELD + RING, 512], F32))
        spill = nc.dram_tensor("spill", (NB, 2, P, 3, T), BF16, kind="Internal").ap()
        acc = ctx.enter_context(nc.psum_tensor("acc", [P, 512], F32))

        cf = sb("cf", [P, CAUS, P])
        cb = sb("cb", [P, N_CONST, P], BF16)
        identf, identb = cf[:, IDENT, :], cb[:, IDENT, :]
        Wm = sb("Wm", [P, 3 * D])
        WoE = sb("WoE", [P, 2, D])
        dirs = sb("dirs", [P, MH, 3])
        hsc = sb("hsc", [P, MH])
        wdot = sb("wdot", [P, MH, 3])
        wgeo = sb("wgeo", [P, 2, MH])
        wgd = sb("wgd", [P, MH, 3])
        Wk2 = sb("Wk2", [P, D])
        Wf = sb("Wf", [P, DEPTH, 3 * INNER])
        Wo = sb("Wo", [P, DEPTH, NP, D])
        W1 = sb("W1", [P, DEPTH, 2 * HID])
        W2 = sb("W2", [P, DEPTH, len(CH), D])
        col = sb("col", [P, DEPTH, 3 + 2 * len(CH)])
        qs = sb("qs", [P, DEPTH, 2, FD])
        rt = sb("rt", [P, DEPTH, 4, NT, FD])

        xtok = sb("xtok", [P, NB, NT, D])
        bst = sb("bst", [P, NB, NT, 6])
        bag = sb("bag", [P, NB, NT, 2])
        vpe = sb("vpe", [P, NB, NT])
        rsx = sb("rsx", [P, NB, NT])
        xT = sb("xT", [P, NB, T])
        hT = sb("hT", [P, NB, T])
        stq = sb("stq", [P, NB, MH, T], BF16)
        stk = sb("stk", [P, NB, MH, T], BF16)
        mv = sb("mv", [P, NB, NT, MH, 32])
        mmx = sb("mmx", [P, NB, NT, MH])
        mmr = sb("mmr", [P, NB, NT * MH])
        mm3 = sb("mm3", [P, NB, P], BF16)
        mmT = sb("mmT", [P, NB, P], BF16)
        pm = sb("pm", [P, NPM, 512])
        oraw = sb("oraw", [P, 2, 512])
        mrec = sb("mrec", [P, 512])
        aT = sb("aT", [P, NB, T])
        sq = sb("sq", [P, 2 * FH, FD])
        ss = sb("ss", [P, 2, 2 * FH])
        ssc = sb("ssc", [P, 2, 2 * FH])
        rn = sb("rn", [P, 2, 2 * FH])
        qkn = sb("qkn", [P, 2, 2 * FH, FD])
        qk = sb("qk", [P, 2 * FH, FD])
        rs = sb("rs", [P, 2 * FH, FD])
        bdq = sb("bdq", [P, 2, NP, 2, 2, WIN])
        kT = sb("kT", [P, NP, WIN + T])
        va = sb("va", [P, NT, FH, FD])
        ve = sb("ve", [P, NT, FH, FD])
        wmx = sb("wmx", [P, 2, 2 * NP])
        pw = sb("pw", [P, 2, NP, P])
        wsum = sb("wsum", [P, 2, 2 * NP])
        wrec = sb("wrec", [P, 2, 2 * NP])
        pT = sb("pT", [P, 2, NP, 2, WIN])
        oT = sb("oT", [P, NP, T])
        hc = sb("hc", [P, T])
        hq = sb("hq", [P, T])
        vl = sb("vl", [P, NT])
        rl = sb("rl", [P, NT])
        mhalf = sb("mhalf", [P, 2 * FH])
        gl = sb("gl", [P, len(CH), T])
        xn = pT[:, :, :, :, :].rearrange("p w c a i -> p (w c a i)").rearrange("p (b t d) -> p b t d", b=NB, t=NT)
        yo = xn
        part = pm[:, :, :].rearrange("p k n -> p (k n)")[:, 0:NB * 3 * T].bitcast(BF16)\
            .rearrange("p (b w r n) -> p b w r n", b=NB, w=2, r=3)
        rest = gl
        staged = pm[:, :, :].rearrange("p k n -> p (k n)")[:, 0:(N_CONST - CAUS) * P]\
            .rearrange("p (c n) -> p c n", n=P)
        rp = oT[:, :, :].rearrange("p c n -> p (c n)")[:, 0:4 * NT * FD]\
            .rearrange("p (r t d) -> p r t d", r=4, t=NT)

        NG, NCH = len(GROUPS), len(CH)
        s_wclr = sem("wout_cleared")
        s_load = sem("weights_in")
        s_dset = sem("dve_prologue")
        s_pset = sem("pool_prologue")
        go_pool, go_act, go_dve, go_pe = (sem(f"counts_at_zero_{e}") for e in ("pool", "act", "dve", "pe"))
        s_over = sem("turn_over")
        done = {k: sem("pe_" + k) for k in count}
        s_mpv = sem("pe_mpv")
        s_x = [sem(f"x_in{b}") for b in range(NB)]
        s_st = sem("x_stats")
        s_ag = sem("x_mean_var")
        s_vpe = sem("x_var_eps")
        s_rsx = sem("x_rstd")
        s_xn = sem("x_normed")
        s_xT = sem("xT_ready")
        s_x1 = sem("xT_after_attention")
        s_hT = sem("hT_ready")
        s_hs = sem("hT_for_mlp")
        s_p0 = sem("main_part0")
        s_re = sem("main_rest")
        s_p1 = sem("main_part1")
        s_p2 = sem("main_part2")
        s_spill = [sem(f"main_parts_out{b}") for b in range(NB)]
        s_stk = [sem(f"main_stacks_in{b}") for b in range(NB)]
        s_mv = sem("main_v")
        s_mmx = sem("main_max")
        s_mm = sem("main_max_parts")
        s_mmT = sem("main_max_rows")
        s_mst = [sem(f"main_max_in{b}") for b in range(NB)]
        s_pm = sem("main_exp")
        s_or = sem("main_o_raw")
        s_mrec = sem("main_recip")
        s_on = sem("main_o")
        s_aT = sem("main_result")
        s_sq = sem("win_squares")
        s_ss = sem("win_sumsq")
        s_ssc = sem("win_sumsq_clamped")
        s_rn = sem("win_rnorm")
        s_qkn = sem("win_qk_normed")
        s_rc = sem("rope_cos")
        s_rs = sem("rope_sin")
        s_qk = sem("rope_sum")
        s_va = sem("win_v")
        s_ve = [sem(f"win_v_even_in{t}") for t in range(NT)]
        s_bdq = sem("win_qT")
        s_kT = sem("win_kT")
        s_wmx = sem("win_max")
        s_pw = sem("win_exp")
        s_wrec = sem("win_recip")
        s_wn = sem("win_weights")
        s_pT = sem("win_weightsT")
        s_oT = sem("win_oT")
        s_hc = sem("ln_centered")
        s_hq = sem("ln_squares")
        s_vl = sem("ln_var")
        s_rl = sem("ln_rstd")
        s_hu = sem("ln_scaled")
        s_hn = sem("ln_out")
        s_gl = sem("mlp_gelu")
        s_uu = sem("mlp_gated")
        s_y1 = sem("mlp_result")
        s_yT = sem("sum_ready")
        s_yo = sem("rows_ready")
        s_out = [sem(f"stored{b}") for b in range(NB)]
        of_a_turn = range(s_over.num, s_out[-1].num + 1)

        def turn_ends(eng, go):
            eng.drain().then_inc(s_over, 1)
            eng.wait_ge(go, 1)
            eng.sem_clear(go)

        def bank(st, i):
            return ps[:, bank_of[st + (i,)], :]

        def last_read(u):
            kind, a, i = u[0], u[1], u[-1]
            if kind == "xT":
                return s_xT, a + 1
            if kind == "mqkv":
                return (s_re, 2 * a + i + 1) if i < 2 else (s_mv, a + 1)
            if kind == "qkv":
                return (s_qkn, 2 * a + i + 1) if i < 2 else (s_va, a + 1)
            if kind == "ropeT":
                return (s_bdq, 2 * a + 2) if i == 0 else (s_kT, a + 1)
            if kind == "score":
                return s_pw, NP * (2 * a + i + 1)
            if kind == "wT":
                return s_pT, 2 * a + i + 1
            if kind == "pv":
                return s_oT, a + 1
            if kind == "wo":
                return s_x1, a + 1
            if kind == "mean":
                return s_hc, a + 1
            if kind == "var":
                return s_vl, a + 1
            if kind == "rstd":
                return s_hu, a + 1
            if kind == "mlp":
                if i == 2 * NCH:
                    l, bb = GROUPS[a]
                    return (s_xT, NB * (l + 1) + bb + 1) if l + 1 < DEPTH else (s_y1, bb + 1)
                return (s_uu, NCH * a + i // 2 + 1) if i % 2 else (s_gl, NCH * a + i // 2 + 1)
            if kind == "mmax":
                return s_mmx, nth[u] + 1
            if kind == "mmaxT":
                return s_mmT, a + 1
            if kind == "mexp":
                return s_pm, nth[u] + 1
            if kind == "mden":
                return s_mrec, nth[u] + 1
            if kind == "mout":
                return s_aT, a + 1
            assert kind == "yT"
            return s_yo, a + 1

        def emptied(st, i):
            was = before[st + (i,)]
            return last_read(was) if was else (done[st[0]], 0)

        def filled(st, i):
            return done[st[0]], nth[st + (i,)] + 1

        def tile_of(n):
            l, bb, t = TILES[n]
            return l, bb, t, n // NT

        loads = [
            (Wm[:, :], Wqkv),
            (cf[:, :, :], consts[0:CAUS].rearrange("c p n -> p c n")),
            (staged, consts[CAUS:N_CONST].rearrange("c p n -> p c n")),
            (dirs[:, :, :], head_dirs.rearrange("(a h) d -> a h d", a=1).to_broadcast([P, MH, 3])),
            (hsc[:, :], head_scales.rearrange("(a h) -> a h", a=1).to_broadcast([P, MH])),
            (Wf[:, :, :], wqkv.rearrange("l p n -> p l n")),
            (rp[:, :, :, :], rope.rearrange("r (t p) d -> p r t d", p=P)),
            (Wo[:, :, :, :], wo.rearrange("l (c p) n -> p l c n", p=P)),
            (W1[:, :, :], w1.rearrange("l p n -> p l n")),
        ]
        for l in range(DEPTH):
            for i, a in ((0, q_scale), (1, k_scale)):
                loads.append((qs[:, l, i, :], a[l:l + 1, :].to_broadcast([P, FD])))
            for c, (c0, r) in enumerate(CH):
                loads.append((W2[0:r, l, c, :], w2[l, c0:c0 + r, :]))
                loads.append((col[0:r, l, 3 + c:4 + c], b1[l, c0:c0 + r].rearrange("(p a) -> p a", a=1)))
                loads.append((col[0:r, l, 3 + NCH + c:4 + NCH + c],
                              b1[l, HID + c0:HID + c0 + r].rearrange("(p a) -> p a", a=1)))
            for i, a in ((0, ln_g), (1, ln_b), (2, b2)):
                loads.append((col[:, l, i:i + 1], a[l, :].rearrange("(p a) -> p a", a=1)))
        for h in range(MH):
            g, i = h // GH, h % GH
            loads.append((WoE[32 * i:32 * i + MD, g, :], Wout[MD * h:MD * h + MD, :]))
        N_LOADS = len(loads)
        N_DSET, N_PSET = 8, 8 + 8 * DEPTH
        block = ctx.enter_context(nc.Block())

        @block.sync
        def _(sp):
            sp.wait_ge(s_wclr, 1)
            for dst, src in loads:
                sp.dma_start(dst, src).then_inc(s_load, 16)
            sp.wait_ge(s_pset, 7)
            with sp.Fori(0, TURNS) as turn:
                for bb in range(NB):
                    sp.dma_start(xtok[:, bb, :, :], x[turn * NB + bb].rearrange("(t p) d -> p t d", p=P))\
                        .then_inc(s_x[bb], 16)
                for st in steps:
                    kind = st[0]
                    if kind == "mqkv":
                        bb = st[1]
                        for w in range(2):
                            sp.wait_ge(s_p2, 2 * bb + w + 1)
                            sp.dma_start(spill[bb, w], part[:, bb, w, :, :]).then_inc(s_spill[bb], 16)
                        sp.wait_ge(s_spill[bb], 32)
                        for w, stack in enumerate((stq, stk)):
                            for r, term in enumerate(TERMS):
                                sp.dma_start(
                                    stack[MD * r:MD * r + MD, bb, :, :],
                                    spill[bb, w, :, term[w], :].rearrange("(h d) n -> d h n", h=MH))\
                                    .then_inc(s_stk[bb], 16)
                    elif kind == "mmaxT":
                        bb = st[1]
                        sp.wait_ge(s_mmT, bb + 1)
                        for p in range(3):
                            for i in range(NT):
                                r = NT * MH * p + MH * i
                                sp.dma_start(stq[KS + p:KS + p + 1, bb, :, P * i:P * i + P],
                                                 mmT[r:r + MH, bb, :]).then_inc(s_mst[bb], 16)
                    elif kind == "qkv":
                        n = st[1]
                        l, bb, t, gi = tile_of(n)
                        sp.wait_ge(s_va, n + 1)
                        sp.wait_ge(done["pv"], max(0, n - NT + 1))
                        sp.dma_start(ve[0:WIN, t, :, :], va[0:WIN, t, :, :]).then_inc(s_ve[t], 16)
                        if t + 1 < NT:
                            sp.wait_ge(done["pv"], max(0, n - NT + 2))
                            sp.dma_start(ve[WIN:P, t + 1, :, :], va[WIN:P, t, :, :]).then_inc(s_ve[t + 1], 16)
                    elif kind == "yT":
                        bb = st[1]
                        sp.wait_ge(s_yo, bb + 1)
                        sp.dma_start(out[turn * NB + bb].rearrange("(t p) d -> p t d", p=P),
                                         yo[:, bb, :, :]).then_inc(s_out[bb], 16)
                for bb in range(NB):
                    sp.wait_ge(s_out[bb], 16)
                sp.wait_ge(s_over, 4)
                sp.sem_clear(of_a_turn)
                for go in (go_pool, go_act, go_dve, go_pe):
                    sp.drain().then_inc(go, 1)

        @block.gpsimd
        def _(pool):
            pool.memset(WoE[:, :, :], 0.0).then_inc(s_wclr, 1)
            pool.memset(hT[:, :, :], 0.0).then_inc(s_pset, 1)
            pool.memset(bdq[:, :, :, :, :, :], 0.0).then_inc(s_pset, 1)
            pool.memset(kT[:, :, 0:WIN], 0.0).then_inc(s_pset, 1)
            pool.memset(ve[:, 0, :, :], 0.0).then_inc(s_pset, 1)
            pool.memset(mhalf[:, :], -0.5).then_inc(s_pset, 1)
            pool.memset(mm3[:, :, :], 0.0).then_inc(s_pset, 1)
            pool.memset(mv[:, :, :, :, MD:32], 1.0).then_inc(s_pset, 1)
            pool.wait_ge(s_pset, 7)
            pool.memset(stk[KS:P, :, :, :], 1.0).then_inc(s_pset, 1)
            pool.wait_ge(s_pset, 8)
            pool.wait_ge(s_load, 16 * N_LOADS)
            for l in range(DEPTH):
                for w in range(2):
                    for j in range(2):
                        for hf in range(2):
                            a = 32 * (hf if j == 0 else 1 - hf)
                            pool.tensor_tensor(
                                rt[:, l, 2 * w + j, :, 32 * hf:32 * hf + 32],
                                rp[:, 2 * w + j, :, 32 * hf:32 * hf + 32],
                                qs[:, l, w:w + 1, a:a + 32].to_broadcast([P, NT, 32]), ALU.mult)\
                                    .then_inc(s_pset, 1)

            pool.wait_ge(s_pset, N_PSET)
            with pool.Fori(0, TURNS) as turn:
                for st in steps:
                    kind = st[0]
                    if kind == "xT" and st[1] == 0:
                        for bb in range(NB):
                            pool.wait_ge(s_vpe, bb + 1)
                            pool.tensor_tensor(rsx[:, bb, :], vpe[:, bb, :], mhalf[:, 0:NT], ALU.pow)\
                                .then_inc(s_rsx, 1)
                    elif kind == "sums":
                        n = st[1]
                        pool.wait_ge(s_ssc, n + 1)
                        pool.tensor_tensor(rn[:, n % 2, :], ssc[:, n % 2, :], mhalf[:, :], ALU.pow)\
                            .then_inc(s_rn, 1)
                    elif kind == "norm":
                        n = st[1]
                        l, bb, t, gi = tile_of(n)
                        for w in range(2):
                            pool.wait_ge(s_qkn, 2 * n + w + 1)
                            pool.wait_ge(s_qk, n)
                            hs = slice(FH * w, FH * w + FH)
                            for hf in range(2):
                                lo, hi = 32 * hf, 32 * (1 - hf)
                                pool.tensor_tensor(
                                    rs[:, hs, lo:lo + 32], qkn[:, n % 2, hs, hi:hi + 32],
                                    rt[:, l, 2 * w + 1, t:t + 1, lo:lo + 32].to_broadcast([P, FH, 32]),
                                    ALU.mult).then_inc(s_rs, 1)
                    elif kind == "rope":
                        n = st[1]
                        pool.wait_ge(s_rs, 4 * n + 4)
                        pool.wait_ge(s_rc, 2 * n + 2)
                        pool.tensor_tensor(qk[:, :, :], qk[:, :, :], rs[:, :, :], ALU.add).then_inc(s_qk, 1)
                    elif kind == "rstd":
                        gi = st[1]
                        pool.wait_ge(s_vl, gi + 1)
                        pool.wait_ge(done["rstd"], gi)
                        pool.tensor_tensor(rl[:, :], vl[:, :], mhalf[:, 0:NT], ALU.pow).then_inc(s_rl, 1)
                    elif kind == "mean":
                        gi = st[1]
                        bb = GROUPS[gi][1]
                        pool.wait_ge(s_hc, gi + 1)
                        pool.wait_ge(done["var"], gi)
                        pool.tensor_tensor(hq[:, :], hc[:, :], hc[:, :], ALU.mult).then_inc(s_hq, 1)
                    elif kind == "mden":
                        _, bb, g = st
                        k = 2 * bb + g
                        pool.wait_ge(s_mrec, k + 1)
                        pool.tensor_tensor(oraw[:, g, :], oraw[:, g, :], mrec[:, :], ALU.mult).then_inc(s_on, 1)
                turn_ends(pool, go_pool)

        @block.scalar
        def _(act):
            act.wait_ge(s_load, 16 * N_LOADS)
            act.wait_ge(s_pset, 8)

            def shift(bb, s):
                act.activation(hT[0:64, bb, :], xT[0:64, bb, :], ACT.Copy).then_inc(s, 1)
                act.activation(hT[64:P, bb, 1:T], xT[64:P, bb, 0:T - 1], ACT.Copy).then_inc(s, 1)

            with act.Fori(0, TURNS) as turn:
                for st in steps:
                    kind = st[0]
                    if kind == "hT":
                        l, bb = st[1:]
                        act.wait_ge(s_xT, NB * l + bb + 1)
                        if l:
                            act.wait_ge(s_hc, NB * (l - 1) + bb + 1)
                        shift(bb, s_hT)
                    elif kind == "h2":
                        gi = st[1]
                        bb = GROUPS[gi][1]
                        act.wait_ge(s_x1, gi + 1)
                        act.wait_ge(done["qkv"], 3 * NT * (gi + 1))
                        shift(bb, s_hs)
                    elif kind == "mqkv":
                        bb = st[1]
                        for w in range(2):
                            act.wait_ge(*filled(st, w))
                            src = bank(st, w)
                            act.activation(part[:, bb, w, 0, :], src, ACT.Copy).then_inc(s_p0, 1)
                        act.wait_ge(*filled(st, 2))
                        src = bank(st, 2)
                        act.activation(mv[:, bb, :, :, 0:MD],
                                           src.rearrange("p (t h d) -> p t h d", t=NT, h=MH), ACT.Copy)\
                                               .then_inc(s_mv, 1)
                    elif kind == "ropeT":
                        n = st[1]
                        l, bb, t, gi = tile_of(n)
                        act.wait_ge(*filled(st, 0))
                        src = bank(st, 0).rearrange("p (c w i) -> p c w i", c=NP, w=2)
                        act.wait_ge(done["score"], max(0, 2 * (n - 1)))
                        act.activation(bdq[0:64, n % 2, :, :, 0, :], src[0:64], ACT.Copy).then_inc(s_bdq, 1)
                        act.activation(bdq[64:P, n % 2, :, :, 1, :], src[64:P], ACT.Copy).then_inc(s_bdq, 1)
                        act.wait_ge(*filled(st, 1))
                        src = bank(st, 1)
                        act.wait_ge(done["score"], 2 * min(n, NT * gi))
                        act.activation(kT[:, :, WIN + P * t:WIN + P * (t + 1)],
                                           src.rearrange("p (c i) -> p c i", c=NP), ACT.Copy).then_inc(s_kT, 1)
                    elif kind == "qkv":
                        n = st[1]
                        l, bb, t, gi = tile_of(n)
                        for w in range(2):
                            act.wait_ge(*filled(st, w))
                            src = bank(st, w)
                            act.wait_ge(s_ss, n)
                            act.activation(sq[:, FH * w:FH * w + FH, :],
                                               src.rearrange("p (h d) -> p h d", h=FH), ACT.Square)\
                                                   .then_inc(s_sq, 1)
                        act.wait_ge(*filled(st, 2))
                        src = bank(st, 2)
                        act.wait_ge(done["pv"], max(0, n - NT + 1))
                        act.wait_ge(s_ve[t], 16 * (2 if t else 1) * gi)
                        if t + 1 < NT:
                            act.wait_ge(s_ve[t + 1], 16 * 2 * gi)
                        act.activation(va[:, t, :, 0:FD], src.rearrange("p (h d) -> p h d", h=FH),
                                           ACT.Copy).then_inc(s_va, 1)
                    elif kind == "exp":
                        n = st[1]
                        b = n % 2
                        act.wait_ge(done["wT"], 2 * n)
                        for w in range(2):
                            act.wait_ge(s_wmx, 2 * n + w + 1)
                            src = bank(("score", n), w)
                            for c in range(NP):
                                k = NP * w + c
                                act.activation(pw[:, w, c, :], src[:, P * c:P * c + P], ACT.Exp,
                                               bias=wmx[:, b, k:k + 1], accum_out=wsum[:, b, k:k + 1])\
                                    .then_inc(s_pw, 1)
                    elif kind == "wT":
                        n = st[1]
                        for w in range(2):
                            act.wait_ge(*filled(st, w))
                            src = bank(st, w)
                            act.wait_ge(done["pv"], n)
                            act.activation(pT[:, w, :, :, :],
                                           src.rearrange("p (c a i) -> p c a i", c=NP, a=2), ACT.Copy)\
                                .then_inc(s_pT, 1)
                    elif kind == "pv":
                        n = st[1]
                        l, bb, t, gi = tile_of(n)
                        act.wait_ge(*filled(st, 0))
                        src = bank(st, 0)
                        act.wait_ge(done["wo"], gi)
                        act.activation(oT[:, :, P * t:P * t + P],
                                       src.rearrange("p (c i) -> p c i", c=NP), ACT.Copy).then_inc(s_oT, 1)
                    elif kind == "mlp":
                        gi = st[1]
                        l, bb = GROUPS[gi]
                        for c, (c0, r) in enumerate(CH):
                            act.wait_ge(*filled(st, 2 * c))
                            src = bank(st, 2 * c)
                            act.wait_ge(done["mlp"], (2 * NCH + 1) * gi)
                            k = 3 + NCH + c
                            act.activation(gl[0:r, c, :], src[0:r], ACT.Gelu, bias=col[0:r, l, k:k + 1])\
                                .then_inc(s_gl, 1)
                    elif kind == "mexp":
                        _, bb, g, k = st
                        hs, J = exp_units(g)[k]
                        wd = len(hs) * (T - P * J)
                        act.wait_ge(*filled(st, 0))
                        src = bank(st, 0)
                        act.wait_ge(s_mpv, NT * (2 * bb + g) + (k >= NPM))
                        act.activation(pm[:, k % NPM, 0:wd], src[:, 0:wd], ACT.Exp).then_inc(s_pm, 1)
                    elif kind == "mmaxT":
                        bb = st[1]
                        act.wait_ge(*filled(st, 0))
                        src = bank(st, 0)[:, 0:P // 2].bitcast(BF16)
                        act.activation(mmT[:, bb, :], src, ACT.Copy).then_inc(s_mmT, 1)
                    elif kind == "mout":
                        bb = st[1]
                        act.wait_ge(*filled(st, 0))
                        src = bank(st, 0)
                        act.activation(aT[:, bb, :], src, ACT.Copy).then_inc(s_aT, 1)
                turn_ends(act, go_act)

        @block.vector
        def _(dve):
            dve.wait_ge(s_load, 16 * N_LOADS)
            dve.tensor_copy(cb[:, 0:CAUS, :], cf[:, :, :]).then_inc(s_dset, 1)
            dve.tensor_copy(cb[:, CAUS:N_CONST, :], staged).then_inc(s_dset, 1)
            wk = Wm[:, D:2 * D].rearrange("p (h d) -> p h d", h=MH)
            wk2 = Wk2[:, :].rearrange("p (h d) -> p h d", h=MH)
            dve.tensor_tensor(wdot[:, :, :], wk[:, :, 0:3], dirs[:, :, :], ALU.mult).then_inc(s_dset, 1)
            dve.wait_ge(s_dset, 3)
            dve.tensor_reduce(wgeo[:, 0, :], wdot[:, :, :], AX.X, ALU.add).then_inc(s_dset, 1)
            dve.wait_ge(s_dset, 4)
            dve.tensor_tensor(wgeo[:, 1, :], wgeo[:, 0, :], hsc[:, :], ALU.mult).then_inc(s_dset, 1)
            dve.wait_ge(s_dset, 5)
            dve.tensor_tensor(wgd[:, :, :], dirs[:, :, :],
                                  wgeo[:, 1, :].rearrange("p (h a) -> p h a", a=1).to_broadcast([P, MH, 3]),
                                  ALU.mult).then_inc(s_dset, 1)
            dve.tensor_scalar(Wk2[:, :], Wm[:, D:2 * D], float(MD) ** -0.5, None, ALU.mult).then_inc(s_dset, 1)
            dve.wait_ge(s_dset, 7)
            dve.tensor_tensor(wk2[:, :, 0:3], wk2[:, :, 0:3], wgd[:, :, :], ALU.add).then_inc(s_dset, 1)
            dve.wait_ge(s_pset, N_PSET)

            def split(src, p0, rest_, p1, p2, s, n):
                dve.tensor_copy(p0, src).then_inc(s, 1)
                dve.wait_ge(s, n + 1)
                dve.tensor_tensor(rest_, src, p0, ALU.subtract).then_inc(s, 1)
                dve.wait_ge(s, n + 2)
                dve.tensor_copy(p1, rest_).then_inc(s, 1)
                dve.wait_ge(s, n + 3)
                dve.tensor_tensor(p2, rest_, p1, ALU.subtract).then_inc(s, 1)

            with dve.Fori(0, TURNS) as turn:
                for st in steps:
                    kind = st[0]
                    if kind == "xT":
                        bb = st[1]
                        if bb == 0:
                            for c in range(NB):
                                dve.wait_ge(s_x[c], 16)
                                for t in range(NT):
                                    dve.bn_stats(bst[:, c, t, :], xtok[:, c, t, :]).then_inc(s_st, 1)
                                dve.wait_ge(s_st, NT * (c + 1))
                                for t in range(NT):
                                    dve.bn_aggr(bag[:, c, t, :], bst[:, c, t, :]).then_inc(s_ag, 1)
                                dve.wait_ge(s_ag, NT * (c + 1))
                                dve.tensor_scalar(vpe[:, c, :], bag[:, c, :, 1], EPS, None, ALU.add)\
                                    .then_inc(s_vpe, 1)
                            for c in range(NB):
                                dve.wait_ge(s_rsx, c + 1)
                                for t in range(NT):
                                    dve.tensor_scalar(xn[:, c, t, :], xtok[:, c, t, :], bag[:, c, t, 0:1],
                                                          rsx[:, c, t:t + 1], ALU.subtract, ALU.mult)\
                                                              .then_inc(s_xn, 1)
                        dve.wait_ge(*filled(st, 0))
                        src = bank(st, 0)
                        dve.tensor_copy(xT[:, bb, :], src).then_inc(s_xT, 1)
                    elif kind == "mqkv":
                        bb = st[1]
                        for w in range(2):
                            i = 2 * bb + w
                            dve.wait_ge(*filled(st, w))
                            src = bank(st, w)
                            dve.wait_ge(s_p0, i + 1)
                            dve.wait_ge(s_p2, max(0, i - 1))
                            dve.tensor_tensor(rest[:, w, :], src, part[:, bb, w, 0, :], ALU.subtract)\
                                .then_inc(s_re, 1)
                            dve.wait_ge(s_re, i + 1)
                            dve.tensor_copy(part[:, bb, w, 1, :], rest[:, w, :]).then_inc(s_p1, 1)
                            dve.wait_ge(s_p1, i + 1)
                            dve.tensor_tensor(part[:, bb, w, 2, :], rest[:, w, :], part[:, bb, w, 1, :],
                                                  ALU.subtract).then_inc(s_p2, 1)
                    elif kind == "sums":
                        n = st[1]
                        b = n % 2
                        dve.wait_ge(s_sq, 2 * n + 2)
                        dve.tensor_reduce(ss[:, b, :], sq[:, :, :], AX.X, ALU.add).then_inc(s_ss, 1)
                        dve.wait_ge(s_ss, n + 1)
                        dve.tensor_scalar(ssc[:, b, :], ss[:, b, :], 1e-24, None, ALU.max).then_inc(s_ssc, 1)
                    elif kind == "norm":
                        n = st[1]
                        b = n % 2
                        for w in range(2):
                            hs = slice(FH * w, FH * w + FH)
                            src = bank(("qkv", n), w).rearrange("p (h d) -> p h d", h=FH)
                            dve.wait_ge(s_rn, n + 1)
                            dve.wait_ge(s_rs, max(0, 4 * (n - 1)))
                            dve.tensor_tensor(
                                qkn[:, b, hs, :], src,
                                rn[:, b, hs].rearrange("p (h a) -> p h a", a=1).to_broadcast([P, FH, FD]),
                                ALU.mult).then_inc(s_qkn, 1)
                    elif kind == "rope":
                        n = st[1]
                        l, bb, t, gi = tile_of(n)
                        for w in range(2):
                            hs = slice(FH * w, FH * w + FH)
                            dve.wait_ge(s_qkn, 2 * n + w + 1)
                            dve.wait_ge(done["ropeT"], 2 * n)
                            dve.tensor_tensor(
                                qk[:, hs, :], qkn[:, n % 2, hs, :],
                                rt[:, l, 2 * w, t:t + 1, :].to_broadcast([P, FH, FD]), ALU.mult)\
                                .then_inc(s_rc, 1)
                    elif kind == "score":
                        n = st[1]
                        b = n % 2
                        for w in range(2):
                            dve.wait_ge(*filled(st, w))
                            src = bank(st, w).rearrange("p (c j) -> p c j", c=NP)
                            dve.wait_ge(s_pw, max(0, 2 * NP * (n - 1)))
                            dve.tensor_reduce(wmx[:, b, NP * w:NP * w + NP], src, AX.X, ALU.max,
                                              negate=True).then_inc(s_wmx, 1)
                    elif kind == "weights":
                        n = st[1]
                        b = n % 2
                        for w in range(2):
                            ks = slice(NP * w, NP * w + NP)
                            dve.wait_ge(s_pw, NP * (2 * n + w + 1))
                            dve.wait_ge(s_wn, max(0, 2 * n + w - 3))
                            dve.reciprocal(wrec[:, b, ks], wsum[:, b, ks]).then_inc(s_wrec, 1)
                            dve.wait_ge(s_wrec, 2 * n + w + 1)
                            dve.tensor_tensor(
                                pw[:, w, :, :], pw[:, w, :, :],
                                wrec[:, b, ks].rearrange("p (c a) -> p c a", a=1).to_broadcast([P, NP, P]),
                                ALU.mult).then_inc(s_wn, 1)
                    elif kind == "wo":
                        gi = st[1]
                        l, bb = GROUPS[gi]
                        dve.wait_ge(*filled(st, 0))
                        src = bank(st, 0)
                        dve.wait_ge(s_hT, 2 * (NB * l + bb) + 2)
                        dve.wait_ge(done["mqkv"], 3 * NB)
                        dve.tensor_tensor(xT[:, bb, :], src, xT[:, bb, :], ALU.add).then_inc(s_x1, 1)
                    elif kind == "mean":
                        gi = st[1]
                        bb = GROUPS[gi][1]
                        dve.wait_ge(*filled(st, 0))
                        src = bank(st, 0)
                        dve.wait_ge(done["mlp"], (2 * NCH + 1) * gi)
                        dve.tensor_tensor(hc[:, :], hT[:, bb, :], src, ALU.subtract).then_inc(s_hc, 1)
                    elif kind == "var":
                        gi = st[1]
                        dve.wait_ge(*filled(st, 0))
                        src = bank(st, 0)
                        dve.wait_ge(s_rl, gi)
                        dve.tensor_scalar(vl[:, :], src[:, 0:NT], EPS, None, ALU.add).then_inc(s_vl, 1)
                    elif kind == "rstd":
                        gi = st[1]
                        l, bb = GROUPS[gi]
                        dve.wait_ge(*filled(st, 0))
                        src = bank(st, 0)
                        dve.wait_ge(s_hq, gi + 1)
                        dve.tensor_tensor(hc[:, :], hc[:, :], src, ALU.mult).then_inc(s_hu, 1)
                        dve.wait_ge(s_hu, gi + 1)
                        dve.tensor_scalar(hc[:, :], hc[:, :], col[:, l, 0:1], col[:, l, 1:2],
                                          ALU.mult, ALU.add).then_inc(s_hn, 1)
                    elif kind == "mlp":
                        gi = st[1]
                        l, bb = GROUPS[gi]
                        for c, (c0, r) in enumerate(CH):
                            dve.wait_ge(*filled(st, 2 * c + 1))
                            src = bank(st, 2 * c + 1)
                            dve.wait_ge(s_gl, NCH * gi + c + 1)
                            dve.scalar_tensor_tensor(out=gl[0:r, c, :], in0=src[0:r],
                                                         scalar=col[0:r, l, 3 + c:4 + c], in1=gl[0:r, c, :],
                                                         op0=ALU.add, op1=ALU.mult).then_inc(s_uu, 1)
                        dve.wait_ge(*filled(st, 2 * NCH))
                        src = bank(st, 2 * NCH)
                        dve.wait_ge(s_hs, 2 * gi + 2)
                        dve.scalar_tensor_tensor(out=xT[:, bb, :], in0=src, scalar=col[:, l, 2:3],
                                                     in1=xT[:, bb, :], op0=ALU.add, op1=ALU.add)\
                                                         .then_inc(s_xT if l + 1 < DEPTH else s_y1, 1)
                    elif kind == "mmax":
                        _, bb, g, k = st
                        hs, I = max_units(g)[k]
                        wd = P * (I + 1)
                        dve.wait_ge(*filled(st, 0))
                        src = bank(st, 0)[:, 0:len(hs) * wd].rearrange("p (h j) -> p h j", j=wd)
                        dve.tensor_reduce(mmx[:, bb, I, hs[0]:hs[-1] + 1], src, AX.X, ALU.max,
                                              negate=True).then_inc(s_mmx, 1)
                    elif kind == "mmaxT":
                        bb = st[1]
                        dve.wait_ge(s_mmx, 2 * NU * (bb + 1))
                        k = NT * MH
                        split(mmx[:, bb, :, :].rearrange("p i h -> p (i h)"), mm3[:, bb, 0:k],
                              mmr[:, bb, :], mm3[:, bb, k:2 * k], mm3[:, bb, 2 * k:3 * k], s_mm, 4 * bb)
                    elif kind == "mden":
                        _, bb, g = st
                        k = 2 * bb + g
                        dve.wait_ge(s_mpv, NT * (k + 1))
                        dve.wait_ge(s_on, k)
                        dve.wait_ge(done["mout"], bb)
                        dve.tensor_copy(oraw[:, g, :], acc[:, :]).then_inc(s_or, 1)
                        dve.wait_ge(*filled(st, 0))
                        src = bank(st, 0)
                        dve.reciprocal(mrec[:, :], src).then_inc(s_mrec, 1)
                    elif kind == "yT":
                        bb = st[1]
                        dve.wait_ge(s_aT, bb + 1)
                        dve.wait_ge(s_y1, bb + 1)
                        dve.tensor_tensor(aT[:, bb, :], xT[:, bb, :], aT[:, bb, :], ALU.add).then_inc(s_yT, 1)
                        dve.wait_ge(*filled(st, 0))
                        src = bank(st, 0)
                        dve.tensor_tensor(yo[:, bb, :, :].rearrange("p t d -> p (t d)"), src,
                                              xtok[:, bb, :, :].rearrange("p t d -> p (t d)"), ALU.add)\
                                                  .then_inc(s_yo, 1)
                turn_ends(dve, go_dve)

        @block.tensor
        def _(pe):
            pe.wait_ge(s_load, 16 * N_LOADS)
            pe.wait_ge(s_dset, N_DSET)
            pe.wait_ge(s_pset, N_PSET)

            def mm(o, a, b, start=True, stop=True):
                return pe.matmul(o, a, b, start=start, stop=stop)

            with pe.Fori(0, TURNS) as turn:
                for st in steps:
                    kind = st[0]
                    if kind == "xT":
                        bb = st[1]
                        pe.wait_ge(*emptied(st, 0))
                        o = bank(st, 0)
                        pe.wait_ge(s_xn, NT * (bb + 1))
                        for t in range(NT):
                            i = pe.transpose(o[:, P * t:P * t + P], xn[:, bb, t, :], identf)
                        i.then_inc(done[kind], 1)
                    elif kind == "mqkv":
                        bb = st[1]
                        pe.wait_ge(s_xT, bb + 1)
                        pe.wait_ge(*emptied(st, 0))
                        mm(bank(st, 0), Wm[:, 0:D], xT[:, bb, :]).then_inc(done[kind], 1)
                        pe.wait_ge(*emptied(st, 1))
                        mm(bank(st, 1), Wk2[:, :], xT[:, bb, :]).then_inc(done[kind], 1)
                        pe.wait_ge(*emptied(st, 2))
                        o = bank(st, 2)
                        for t in range(NT):
                            i = mm(o[:, P * t:P * t + P], xT[:, bb, P * t:P * t + P], Wm[:, 2 * D:3 * D])
                        i.then_inc(done[kind], 1)
                    elif kind == "qkv":
                        n = st[1]
                        l, bb, t, gi = tile_of(n)
                        pe.wait_ge(s_hT, 2 * (NB * l + bb) + 2)
                        for w in range(3):
                            pe.wait_ge(*emptied(st, w))
                            o = bank(st, w)
                            mm(o, hT[:, bb, P * t:P * t + P], Wf[:, l, INNER * w:INNER * (w + 1)])\
                                .then_inc(done[kind], 1)
                    elif kind == "ropeT":
                        n = st[1]
                        pe.wait_ge(s_qk, n + 1)
                        for w in range(2):
                            pe.wait_ge(*emptied(st, w))
                            o = bank(st, w)
                            for c in range(NP):
                                h = FH * w + 2 * c
                                i = pe.transpose(o[:, P * c:P * c + P],
                                                 qk[:, h:h + 2, :].rearrange("p h d -> p (h d)"), identf)
                            i.then_inc(done[kind], 1)
                    elif kind == "score":
                        n = st[1]
                        l, bb, t, gi = tile_of(n)
                        pe.wait_ge(s_bdq, 2 * n + 2)
                        pe.wait_ge(s_kT, n + 1)
                        for w in range(2):
                            pe.wait_ge(*emptied(st, w))
                            o = bank(st, w)
                            m = WIN1 if w else (WINE if t else WIN0)
                            mm(o, identb, cb[:, m:m + 1, :].to_broadcast([P, NP, P]), True, False)
                            for c in range(NP):
                                k0 = P * t + WIN * w
                                q = bdq[:, n % 2, c, w, :, :].rearrange("p a i -> p (a i)")
                                oc = o[:, P * c:P * c + P]
                                if w:
                                    i = mm(oc, q, kT[:, c, k0:k0 + P], False, c == NP - 1)
                                else:
                                    mm(oc[:, 0:WIN], q, kT[:, c, k0 + WIN:k0 + P], False, False)
                                    i = mm(oc[:, WIN:P], q, kT[:, c, k0:k0 + WIN], False, c == NP - 1)
                            i.then_inc(done[kind], 1)
                    elif kind == "wT":
                        n = st[1]
                        for w in range(2):
                            pe.wait_ge(*emptied(st, w))
                            o = bank(st, w)
                            pe.wait_ge(s_wn, 2 * n + w + 1)
                            for c in range(NP):
                                i = pe.transpose(o[:, P * c:P * c + P], pw[:, w, c, :], identf)
                            i.then_inc(done[kind], 1)
                    elif kind == "pv":
                        n = st[1]
                        l, bb, t, gi = tile_of(n)
                        pe.wait_ge(s_pT, 2 * n + 2)
                        pe.wait_ge(s_va, n + 1)
                        pe.wait_ge(s_ve[t], 16 * (2 if t else 1) * (gi + 1))
                        pe.wait_ge(*emptied(st, 0))
                        o = bank(st, 0)
                        for c in range(NP):
                            for w, v in ((0, ve), (1, va)):
                                for a in range(2):
                                    i0 = P * c + WIN * w
                                    i = mm(o[FD * a:FD * a + FD, i0:i0 + WIN], v[:, t, 2 * c + a, :],
                                           pT[:, w, c, a, :])
                        i.then_inc(done[kind], 1)
                    elif kind == "wo":
                        gi = st[1]
                        l, bb = GROUPS[gi]
                        pe.wait_ge(*emptied(st, 0))
                        o = bank(st, 0)
                        pe.wait_ge(s_oT, NT * (gi + 1))
                        for c in range(NP):
                            i = mm(o, Wo[:, l, c, :], oT[:, c, :], c == 0, c == NP - 1)
                        i.then_inc(done[kind], 1)
                    elif kind == "mean":
                        gi = st[1]
                        bb = GROUPS[gi][1]
                        pe.wait_ge(*emptied(st, 0))
                        o = bank(st, 0)
                        pe.wait_ge(s_hs, 2 * gi + 2)
                        mm(o, cf[:, MEAN, :], hT[:, bb, :]).then_inc(done[kind], 1)
                    elif kind == "var":
                        gi = st[1]
                        pe.wait_ge(*emptied(st, 0))
                        o = bank(st, 0)
                        pe.wait_ge(s_hq, gi + 1)
                        for t in range(NT):
                            i = mm(o[:, t:t + 1], hq[:, P * t:P * t + P], cf[:, MEAN, 0:1])
                        i.then_inc(done[kind], 1)
                    elif kind == "rstd":
                        gi = st[1]
                        pe.wait_ge(*emptied(st, 0))
                        o = bank(st, 0)
                        pe.wait_ge(s_rl, gi + 1)
                        for t in range(NT):
                            i = mm(o[:, P * t:P * t + P], rl[:, t:t + 1].to_broadcast([P, P]), identf)
                        i.then_inc(done[kind], 1)
                    elif kind == "mlp":
                        gi = st[1]
                        l, bb = GROUPS[gi]
                        pe.wait_ge(s_hn, gi + 1)
                        for c, (c0, r) in enumerate(CH):
                            for i, first in ((0, HID + c0), (1, c0)):
                                pe.wait_ge(*emptied(st, 2 * c + i))
                                o = bank(st, 2 * c + i)
                                mm(o[0:r], W1[:, l, first:first + r], hc[:, :]).then_inc(done[kind], 1)
                        pe.wait_ge(*emptied(st, 2 * NCH))
                        o = bank(st, 2 * NCH)
                        for c, (c0, r) in enumerate(CH):
                            pe.wait_ge(s_uu, NCH * gi + c + 1)
                            i = mm(o, W2[0:r, l, c, :], gl[0:r, c, :], c == 0, c == NCH - 1)
                        i.then_inc(done[kind], 1)
                    elif kind == "mmax":
                        _, bb, g, k = st
                        hs, I = max_units(g)[k]
                        wd = P * (I + 1)
                        pe.wait_ge(*emptied(st, 0))
                        o = bank(st, 0)
                        pe.wait_ge(s_stk[bb], 16 * 2 * len(TERMS))
                        for j, h in enumerate(hs):
                            mm(o[:, wd * j:wd * (j + 1)], stq[0:KS, bb, h, P * I:P * I + P],
                               stk[0:KS, bb, h, 0:wd], True, False)
                            i = mm(o[:, wd * j + P * I:wd * (j + 1)], identb, cb[:, CAUS, :], False, True)
                        i.then_inc(done[kind], 1)
                    elif kind == "mmaxT":
                        bb = st[1]
                        pe.wait_ge(*emptied(st, 0))
                        o = bank(st, 0)
                        pe.wait_ge(s_mm, 4 * bb + 4)
                        pe.transpose(o[:, 0:P // 2].bitcast(BF16), mm3[:, bb, :], identb)\
                            .then_inc(done[kind], 1)
                    elif kind == "mexp":
                        _, bb, g, k = st
                        hs, J = exp_units(g)[k]
                        wd = T - P * J
                        pe.wait_ge(*emptied(st, 0))
                        o = bank(st, 0)
                        pe.wait_ge(s_mst[bb], 16 * 3 * NT)
                        for j, h in enumerate(hs):
                            mm(o[:, wd * j:wd * (j + 1)], stk[0:KM, bb, h, P * J:P * J + P],
                               stq[0:KM, bb, h, P * J:T], True, False)
                            i = mm(o[:, wd * j:wd * j + P], identb, cb[:, CAUST, :], False, True)
                        i.then_inc(done[kind], 1)
                    elif kind == "mpv":
                        _, bb, g, J = st
                        wd = T - P * J
                        n = 2 * bb + g
                        pe.wait_ge(s_mv, bb + 1)
                        if J == 0:
                            pe.wait_ge(s_or, n)
                        for k in UNITS_OF_J[J]:
                            pe.wait_ge(s_pm, NU * n + k + 1)
                        for k in UNITS_OF_J[J]:
                            for j, h in enumerate(exp_units(g)[k][0]):
                                p0 = 32 * (h % GH)
                                i = mm(acc[p0:p0 + 32, P * J:T], mv[:, bb, J, h, :],
                                       pm[:, k % NPM, wd * j:wd * (j + 1)], J == 0, J == NT - 1)
                        i.then_inc(s_mpv, 1)
                    elif kind == "mden":
                        _, bb, g = st
                        pe.wait_ge(*emptied(st, 0))
                        o = bank(st, 0)
                        pe.wait_ge(s_or, 2 * bb + g + 1)
                        mm(o, cf[:, DEN, :], oraw[:, g, :]).then_inc(done[kind], 1)
                    elif kind == "mout":
                        bb = st[1]
                        pe.wait_ge(*emptied(st, 0))
                        o = bank(st, 0)
                        pe.wait_ge(s_on, 2 * bb + 2)
                        for g in range(2):
                            i = mm(o, WoE[:, g, :], oraw[:, g, :], g == 0, g == 1)
                        i.then_inc(done[kind], 1)
                    elif kind == "yT":
                        bb = st[1]
                        pe.wait_ge(*emptied(st, 0))
                        o = bank(st, 0)
                        pe.wait_ge(s_yT, bb + 1)
                        for t in range(NT):
                            i = pe.transpose(o[:, P * t:P * t + P], aT[:, bb, P * t:P * t + P], identf)
                        i.then_inc(done[kind], 1)
                turn_ends(pe, go_pe)


_INS = ["L0_attn_x", "L0_attn_Wqkv", "L0_attn_Wout", "L0_attn_head_scales", "L0_attn_head_dirs", "L0_ffn_wqkv",
        "L0_ffn_q_scale", "L0_ffn_k_scale", "L0_ffn_wo", "L0_ffn_ln_g", "L0_ffn_ln_b", "L0_ffn_w1", "L0_ffn_b1",
        "L0_ffn_w2", "L0_ffn_b2"]


def kernel(**inputs):
    import numpy as _np
    import concourse.bacc as _bacc
    from concourse import mybir as _mybir
    from concourse.bass_utils import run_bass_kernel_spmd as _run

    nc = _bacc.Bacc("TRN2", target_bir_lowering=False, num_devices=1)
    arrays, args = {}, []
    given = [(n, _np.ascontiguousarray(inputs[n])) for n in _INS] + list(zip(("consts", "rope"), constants()))
    for name, a in given:
        arrays[f"in_{name}_dram"] = a
        args.append(nc.dram_tensor(f"in_{name}_dram", a.shape, _mybir.dt.from_np(a.dtype),
                                   kind="ExternalInput").ap())
    args.append(nc.dram_tensor("out_0_dram", (B, T, D), _mybir.dt.float32, kind="ExternalOutput").ap())
    build(nc, *args)
    r = _run(nc, [arrays], core_ids=[0])
    return r.results[0]["out_0_dram"]
```

```python
from contextlib import ExitStack

import numpy as np

import concourse.bass as bass
from concourse import mybir

F32 = mybir.dt.float32
BF16 = mybir.dt.bfloat16
ALU = mybir.AluOpType
ACT = mybir.ActivationFunctionType
AX = mybir.AxisListType

P = 128
B, T, D = 4, 512, 128
NT = T // P
EPS = 1e-5
NEG = -1e30

MH, MD = 8, 16
GH = 4
TERMS = [(0, 0), (0, 1), (0, 2), (1, 0), (1, 1), (2, 0)]
KS = MD * len(TERMS)
KM = KS + 3

DEPTH, FH, FD, WIN = 2, 8, 64, 64
INNER = FH * FD
NP = FH // 2
HID = int(D * 4 * 2 / 3)
CH = [(c, min(P, HID - c)) for c in range(0, HID, P)]
QK_SCALE = 8.0

NB = 2
TURNS = B // NB
GROUPS = [(l, bb) for l in range(DEPTH) for bb in range(NB)]
TILES = [(l, bb, t) for l, bb in GROUPS for t in range(NT)]
NTL = len(TILES)
HELD, RING = 2, 5

def max_units(g):
    h = GH * g
    return ([([h + i], 3) for i in range(4)] + [([h + i], 2) for i in range(4)]
            + [([h, h + 1], 1), ([h + 2, h + 3], 1), ([h, h + 1, h + 2, h + 3], 0)])


def exp_units(g):
    h = GH * g
    return ([([h + i], 0) for i in range(4)] + [([h + i], 1) for i in range(4)]
            + [([h, h + 1], 2), ([h + 2, h + 3], 2), ([h, h + 1, h + 2, h + 3], 3)])


NPM = 8
NU = 11
UNITS_OF_J = [range(0, 4), range(4, 8), range(8, 10), range(10, 11)]

FIRST_FILL = 3
SLOT = (("qkv", 0), ("wT", 2), ("sums", 0), ("fill", 0), ("norm", 0), ("ropeT", 1), ("pv", 2), ("rope", 0),
        ("tail", 0), ("fill", 2), ("score", 1), ("exp", 1), ("fill", 1), ("weights", 1), ("tail", 1))
TAIL = (("wo", 2, 0), ("h2", 2, 0), ("mean", 2, 1), ("var", 3, 0), ("rstd", 3, 1), ("mlp", 4, 0))
FILL = (3, 3, 1)
LAST_FILL = 6


def fillers():
    out = []
    for bb in range(NB):
        out += [("mmax", bb, g, k) for g in range(2) for k in range(NU)] + [("mmaxT", bb)]
    end = []
    for bb in range(NB):
        for g in range(2):
            for k in range(6):
                out += [("mexp", bb, g, k)]
                if k in (1, 5):
                    out += end[:1]
                    del end[:1]
            out += [("mpv", bb, g, 0)] + [("mexp", bb, g, k) for k in range(6, 10)] + [("mpv", bb, g, 1)]
            out += end + [("mexp", bb, g, 10), ("mpv", bb, g, 2), ("mpv", bb, g, 3), ("mcopy", bb, g)]
            end = [("mden", bb, g), ("mscale", bb, g)]
            if g:
                end += [("mout", bb)]
    return out + end


def order():
    out = [("xT", 0), ("hT", 0, 0)]
    fill = fillers()
    late = {}
    for gi, (l, bb) in enumerate(GROUPS):
        for what, after, place in TAIL:
            at = NT * gi + NT - 1 + after, place
            late.setdefault(at, []).append((what, gi))
            if what == "mlp" and l + 1 < DEPTH:
                late[at].append(("hT", l + 1, bb))
    for s in range(NTL + 2):
        for what, i in SLOT:
            if what == "fill":
                if s >= FIRST_FILL:
                    out += fill[:FILL[i]]
                    del fill[:FILL[i]]
            elif what == "tail":
                out += late.pop((s, i), [])
            elif 0 <= s - i < NTL:
                out.append((what, s - i))
                if (what, s) == ("sums", 0):
                    out += [x for bb in range(1, NB) for x in (("xT", bb), ("hT", 0, bb))]
                if what == "norm" and s < NB:
                    out.append(("mqkv", s))
    for at in sorted(late):
        for step in late[at]:
            if step[0] == "mlp":
                out += fill[:-2] + [step] + [("yT", bb) for bb in range(NB - 1)]
                del fill[:-2]
            else:
                out += [step] + fill[:LAST_FILL]
                del fill[:LAST_FILL]
    return out + fill + [("yT", NB - 1)]


UNITS = {"xT": 1, "mqkv": 3, "qkv": 3, "ropeT": 2, "score": 2, "wT": 2, "pv": 1,
         "wo": 1, "mean": 1, "var": 1, "rstd": 1, "mlp": 2 * len(CH) + 1, "yT": 1, "mmax": 1, "mmaxT": 1,
         "mexp": 1, "mpv": 0, "hT": 0, "h2": 0, "sums": 0, "norm": 0, "rope": 0, "exp": 0, "weights": 0,
         "mcopy": 0, "mscale": 0,
         "mden": 1, "mout": 1}

IDENT, MEAN, DEN, CAUS, CAUST, WIN1, WINE, WIN0 = range(8)
N_CONST = WIN0 + 1


def constants():
    m = np.zeros((N_CONST, P, P), np.float32)
    k, n = np.arange(P)[:, None], np.arange(P)[None, :]
    m[IDENT] = k == n
    m[MEAN] = 1.0 / D
    m[DEN] = k == 32 * (n // 32) + MD
    m[CAUS] = np.where(n <= k, 0.0, NEG)
    m[CAUST] = np.where(n >= k, 0.0, NEG)
    i = k % WIN
    win = np.where(np.where(n < WIN, n >= i, n - WIN <= i), 0.0, NEG)
    m[WIN1] = win
    m[WINE] = np.roll(win, WIN, axis=1)
    m[WIN0] = np.where(n < WIN, m[WINE], NEG)
    f = np.float32
    half = np.arange(0, FD, 2).astype(f)
    t = np.arange(T).astype(f)
    freqs = t[:, None] * (f(1.0) / f(10000.0) ** (half / f(FD)))[None, :]
    base = (half + f(0.4 * FD)) / f(1.4 * FD)
    scale = base[None, :] ** ((t - T // 2) / f(WIN // 2))[:, None]
    cos, sin, scale = (np.concatenate([a, a], 1).astype(f) for a in (np.cos(freqs), np.sin(freqs), scale))
    sin[:, :FD // 2] *= -1
    rope = np.stack([cos * scale * f(QK_SCALE), sin * scale * f(QK_SCALE), cos / scale, sin / scale]).astype(f)
    return m, rope


def build(nc, x, Wqkv, Wout, head_scales, head_dirs, wqkv, q_scale, k_scale, wo, ln_g, ln_b, w1, b1, w2, b2,
          consts, rope, out):
    steps = order()
    bank_of, before, nth, count, held, ring = {}, {}, {}, {}, [], []
    for st in steps:
        for i in range(UNITS[st[0]]):
            u = st + (i,)
            nth[u] = count.get(st[0], 0)
            count[st[0]] = nth[u] + 1
            turns, first, size = (held, 0, HELD) if st[0] == "qkv" and i < 2 else (ring, HELD, RING)
            bank_of[u] = first + len(turns) % size
            before[u] = turns[-size] if len(turns) >= size else None
            turns.append(u)

    with ExitStack() as ctx:
        def sb(name, shape, dt=F32):
            return ctx.enter_context(nc.sbuf_tensor(name, shape, dt))

        def sem(name):
            return ctx.enter_context(nc.semaphore(name))

        ps = ctx.enter_context(nc.psum_tensor("ps", [P, HELD + RING, 512], F32))
        spill = nc.dram_tensor("spill", (NB, 2, P, 3, T), BF16, kind="Internal").ap()
        acc = ctx.enter_context(nc.psum_tensor("acc", [P, 512], F32))

        cf = sb("cf", [P, CAUS, P])
        cb = sb("cb", [P, N_CONST, P], BF16)
        identf, identb = cf[:, IDENT, :], cb[:, IDENT, :]
        Wm = sb("Wm", [P, 3 * D])
        WoE = sb("WoE", [P, 2, D])
        dirs = sb("dirs", [P, MH, 3])
        hsc = sb("hsc", [P, MH])
        wdot = sb("wdot", [P, MH, 3])
        wgeo = sb("wgeo", [P, 2, MH])
        wgd = sb("wgd", [P, MH, 3])
        Wk2 = sb("Wk2", [P, D])
        Wf = sb("Wf", [P, DEPTH, 3 * INNER])
        Wo = sb("Wo", [P, DEPTH, NP, D])
        W1 = sb("W1", [P, DEPTH, 2 * HID])
        W2 = sb("W2", [P, DEPTH, len(CH), D])
        col = sb("col", [P, DEPTH, 3 + 2 * len(CH)])
        qs = sb("qs", [P, DEPTH, 2, FD])
        rt = sb("rt", [P, DEPTH, 4, NT, FD])

        xtok = sb("xtok", [P, B, NT, D])
        bst = sb("bst", [P, B, NT, 6])
        bag = sb("bag", [P, B, NT, 2])
        vpe = sb("vpe", [P, B, NT])
        rsx = sb("rsx", [P, B, NT])
        lnx = sb("lnx", [P, 2, NB, NT])
        xT = sb("xT", [P, NB, T])
        hT = sb("hT", [P, NB, T])
        stq = sb("stq", [P, NB, MH, T], BF16)
        stk = sb("stk", [P, NB, MH, T], BF16)
        mv = sb("mv", [P, NB, NT, MH, 32])
        mmx = sb("mmx", [P, NB, NT, MH])
        mmr = sb("mmr", [P, NB, NT * MH])
        mm3 = sb("mm3", [P, NB, P], BF16)
        mmT = sb("mmT", [P, NB, P], BF16)
        pm = sb("pm", [P, NPM, 512])
        oraw = sb("oraw", [P, 2, 512])
        mrec = sb("mrec", [P, 512])
        aT = sb("aT", [P, NB, T])
        sq = sb("sq", [P, 2 * FH, FD])
        ss = sb("ss", [P, 2, 2 * FH])
        ssc = sb("ssc", [P, 2, 2 * FH])
        rn = sb("rn", [P, 2, 2 * FH])
        qkn = sb("qkn", [P, 2 * FH, FD])
        qk = sb("qk", [P, 2 * FH, FD])
        rs = sb("rs", [P, 2 * FH, FD])
        bdq = sb("bdq", [P, 2, NP, 2, 2, WIN])
        kT = sb("kT", [P, NP, 2 * (NT + 1), WIN])
        va = sb("va", [P, NT, FH, FD])
        ve = sb("ve", [P, NT, FH, FD])
        wmx = sb("wmx", [P, 2, 2 * NP])
        pw = sb("pw", [P, 2, NP, P])
        wsum = sb("wsum", [P, 2, 2 * NP])
        wrec = sb("wrec", [P, 2, 2 * NP])
        pT = sb("pT", [P, 2, NP, 2, WIN])
        oT = sb("oT", [P, NP, T])
        hc = sb("hc", [P, T])
        hq = sb("hq", [P, T])
        vl = sb("vl", [P, NT])
        rl = sb("rl", [P, NT])
        wake = sb("wake", [P, 1])
        mhalf = sb("mhalf", [P, B * NT])
        gl = sb("gl", [P, len(CH), T])
        xn = pT[:, :, :, :, :].rearrange("p w c a i -> p (w c a i)").rearrange("p (b t d) -> p b t d", b=NB, t=NT)
        yo = xn
        part = pm[:, :, :].rearrange("p k n -> p (k n)")[:, 0:NB * 3 * T].bitcast(BF16)\
            .rearrange("p (b w r n) -> p b w r n", b=NB, w=2, r=3)
        rest = gl
        staged = pm[:, :, :].rearrange("p k n -> p (k n)")[:, 0:(N_CONST - CAUS) * P]\
            .rearrange("p (c n) -> p c n", n=P)
        rp = oT[:, :, :].rearrange("p c n -> p (c n)")[:, 0:4 * NT * FD]\
            .rearrange("p (r t d) -> p r t d", r=4, t=NT)

        NG, NCH = len(GROUPS), len(CH)
        s_wclr = sem("wout_cleared")
        s_first = sem("first_in")
        s_main = sem("main_in")
        s_rope = sem("rope_in")
        s_wf = sem("win_qkv_in")
        s_rest = sem("rest_in")
        s_tab = sem("rope_tables")
        s_x = [sem(f"x_in{b}") for b in range(B)]
        s_st = sem("x_stats")
        s_ag = sem("x_mean_var")
        s_vpe = sem("x_var_eps")
        s_rsx = sem("x_rstd")
        s_ones = sem("ones_set")
        s_bq0 = sem("win_q_cleared")
        s_mm3 = sem("main_max_cleared")
        s_dset = sem("dve_prologue")
        s_pset = sem("pool_prologue")
        go_pool, go_act, go_dve, go_pe = (sem(f"counts_at_zero_{e}") for e in ("pool", "act", "dve", "pe"))
        s_over = sem("turn_over")
        done = {k: sem("pe_" + k) for k in count}
        s_mpv = sem("pe_mpv")
        s_ln = sem("x_stats_of_turn")
        s_wake = sem("act_awake")
        s_xn = sem("x_normed")
        s_xT = sem("xT_ready")
        s_x1 = sem("xT_after_attention")
        s_hT = sem("hT_ready")
        s_hs = sem("hT_for_mlp")
        s_p0 = sem("main_part0")
        s_re = sem("main_rest")
        s_p1 = sem("main_part1")
        s_p2 = sem("main_part2")
        s_spill = [sem(f"main_parts_out{b}") for b in range(NB)]
        s_stk = [sem(f"main_stacks_in{b}") for b in range(NB)]
        s_mv = sem("main_v")
        s_mmx = sem("main_max")
        s_mm = sem("main_max_parts")
        s_mmT = sem("main_max_rows")
        s_mst = [sem(f"main_max_in{b}") for b in range(NB)]
        s_pm = sem("main_exp")
        s_or = sem("main_o_raw")
        s_mrec = sem("main_recip")
        s_on = sem("main_o")
        s_aT = sem("main_result")
        s_sq = sem("win_squares")
        s_ss = sem("win_sumsq")
        s_ssc = sem("win_sumsq_clamped")
        s_rn = sem("win_rnorm")
        s_qkn = sem("win_qk_normed")
        s_rc = sem("rope_cos")
        s_rs = sem("rope_sin")
        s_qk = sem("rope_sum")
        s_va = sem("win_v")
        s_ve = [sem(f"win_v_even_in{t}") for t in range(NT)]
        s_bdq = sem("win_qT")
        s_kT = sem("win_kT")
        s_wmx = sem("win_max")
        s_pw = sem("win_exp")
        s_wrec = sem("win_recip")
        s_wn = sem("win_weights")
        s_pT = sem("win_weightsT")
        s_oT = sem("win_oT")
        s_hc = sem("ln_centered")
        s_hq = sem("ln_squares")
        s_vl = sem("ln_var")
        s_rl = sem("ln_rstd")
        s_hu = sem("ln_scaled")
        s_hn = sem("ln_out")
        s_gl = sem("mlp_gelu")
        s_uu = sem("mlp_gated")
        s_y1 = sem("mlp_result")
        s_yT = sem("sum_ready")
        s_yo = sem("rows_ready")
        s_out = [sem(f"stored{b}") for b in range(NB)]
        of_a_turn = range(s_over.num, s_out[-1].num + 1)

        def turn_ends(eng, go):
            eng.drain().then_inc(s_over, 1)
            eng.wait_ge(go, 1)
            eng.sem_clear(go)

        def bank(st, i):
            return ps[:, bank_of[st + (i,)], :]

        def last_read(u):
            kind, a, i = u[0], u[1], u[-1]
            if kind == "xT":
                return s_xT, a + 1
            if kind == "mqkv":
                return (s_re, 2 * a + i + 1) if i < 2 else (s_mv, a + 1)
            if kind == "qkv":
                return (s_qkn, 2 * a + i + 1) if i < 2 else (s_va, a + 1)
            if kind == "ropeT":
                return (s_bdq, 2 * a + 2) if i == 0 else (s_kT, a + 1)
            if kind == "score":
                return s_pw, NP * (2 * a + i + 1)
            if kind == "wT":
                return s_pT, 2 * a + i + 1
            if kind == "pv":
                return s_oT, a + 1
            if kind == "wo":
                return s_x1, a + 1
            if kind == "mean":
                return s_hc, a + 1
            if kind == "var":
                return s_vl, a + 1
            if kind == "rstd":
                return s_hu, a + 1
            if kind == "mlp":
                if i == 2 * NCH:
                    l, bb = GROUPS[a]
                    return (s_xT, NB * (l + 1) + bb + 1) if l + 1 < DEPTH else (s_y1, bb + 1)
                return (s_uu, NCH * a + i // 2 + 1) if i % 2 else (s_gl, NCH * a + i // 2 + 1)
            if kind == "mmax":
                return s_mmx, nth[u] + 1
            if kind == "mmaxT":
                return s_mmT, a + 1
            if kind == "mexp":
                return s_pm, nth[u] + 1
            if kind == "mden":
                return s_mrec, nth[u] + 1
            if kind == "mout":
                return s_aT, a + 1
            assert kind == "yT"
            return s_yo, a + 1

        def emptied(st, i):
            was = before[st + (i,)]
            return last_read(was) if was else (done[st[0]], 0)

        def filled(st, i):
            return done[st[0]], nth[st + (i,)] + 1

        def tile_of(n):
            l, bb, t = TILES[n]
            return l, bb, t, n // NT

        full_ch = HID // P
        c0, r = CH[-1]
        loads_first = [(cf[:, :, :], consts[0:CAUS].rearrange("c p n -> p c n")), (Wm[:, :], Wqkv)]
        loads_main = [
            (staged, consts[CAUS:N_CONST].rearrange("c p n -> p c n")),
            (dirs[:, :, :], head_dirs.rearrange("(a h) d -> a h d", a=1).to_broadcast([P, MH, 3])),
            (hsc[:, :], head_scales.rearrange("(a h) -> a h", a=1).to_broadcast([P, MH])),
        ]
        loads_rope = [
            (rp[:, :, :, :], rope.rearrange("r (t p) d -> p r t d", p=P)),
            (qs[:, :, 0, :], q_scale.rearrange("(a l) d -> a l d", a=1).to_broadcast([P, DEPTH, FD])),
            (qs[:, :, 1, :], k_scale.rearrange("(a l) d -> a l d", a=1).to_broadcast([P, DEPTH, FD])),
        ]
        loads_rest = [(Wf[:, l, :], wqkv[l]) for l in range(1, DEPTH)]
        loads_rest += [
            (Wo[:, :, :, :], wo.rearrange("l (c p) n -> p l c n", p=P)),
            (W1[:, :, :], w1.rearrange("l p n -> p l n")),
            (W2[0:r, :, full_ch, :], w2[:, c0:HID, :].rearrange("l p n -> p l n")),
        ]
        loads_rest += [(W2[:, l, 0:full_ch, :], w2[l, 0:c0, :].rearrange("(c p) n -> p c n", p=P))
                       for l in range(DEPTH)]
        for i, b in ((3, b1[:, 0:HID]), (3 + NCH, b1[:, HID:2 * HID])):
            for c in range(full_ch):
                loads_rest.append((col[:, :, i + c:i + c + 1],
                                   b[:, P * c:P * c + P].rearrange("l (p a) -> p l a", a=1)))
            loads_rest.append((col[0:r, :, i + full_ch:i + full_ch + 1],
                               b[:, c0:HID].rearrange("l (p a) -> p l a", a=1)))
        for i, a in ((0, ln_g), (1, ln_b), (2, b2)):
            loads_rest.append((col[:, :, i:i + 1], a.rearrange("l (p a) -> p l a", a=1)))
        for h in range(MH):
            g, i = h // GH, h % GH
            loads_rest.append((WoE[32 * i:32 * i + MD, g, :], Wout[MD * h:MD * h + MD, :]))
        two_ones = float(np.array([0x3F803F80], np.uint32).view(np.float32)[0])
        N_DSET, N_TAB, N_PSET = 8, 3 * DEPTH, 5

        def rope_tables(eng, l):
            for j, lo, hi, at in ((0, 0, FD, 0), (1, 0, 32, 32), (1, 32, FD, 0)):
                eng.tensor_tensor(
                    rt[:, l, :, :, :].rearrange("p (w j) t d -> p w j t d", j=2)[:, :, j, :, lo:hi],
                    rp.rearrange("p (w j) t d -> p w j t d", j=2)[:, :, j, :, lo:hi],
                    qs[:, l, :, at:at + hi - lo].rearrange("p w (a d) -> p w a d", a=1)
                    .to_broadcast([P, 2, NT, hi - lo]), ALU.mult).then_inc(s_tab, 1)

        block = ctx.enter_context(nc.Block())

        @block.sync
        def _(sp):
            for dst, src in loads_first:
                sp.dma_start(dst, src).then_inc(s_first, 16)
            sp.wait_ge(s_main, 16 * len(loads_main))
            sp.dma_start(Wf[:, 0, :], wqkv[0]).then_inc(s_wf, 16)
            sp.wait_ge(s_wclr, 1)
            for dst, src in loads_rest:
                sp.dma_start(dst, src, allow_slow_non_contiguous=True).then_inc(s_rest, 16)
            with sp.Fori(0, TURNS) as turn:
                for st in steps:
                    kind = st[0]
                    if kind == "mqkv":
                        bb = st[1]
                        for w in range(2):
                            sp.wait_ge(s_p2, 2 * bb + w + 1)
                            sp.dma_start(spill[bb, w], part[:, bb, w, :, :]).then_inc(s_spill[bb], 16)
                        sp.wait_ge(s_spill[bb], 32)
                        for w, stack in enumerate((stq, stk)):
                            for r, term in enumerate(TERMS):
                                sp.dma_start(
                                    stack[MD * r:MD * r + MD, bb, :, :],
                                    spill[bb, w, :, term[w], :].rearrange("(h d) n -> d h n", h=MH))\
                                    .then_inc(s_stk[bb], 16)
                    elif kind == "mmaxT":
                        bb = st[1]
                        sp.wait_ge(s_mmT, bb + 1)
                        for p in range(3):
                            for i in range(NT):
                                r = NT * MH * p + MH * i
                                sp.dma_start(stq[KS + p:KS + p + 1, bb, :, P * i:P * i + P],
                                                 mmT[r:r + MH, bb, :]).then_inc(s_mst[bb], 16)
                    elif kind == "qkv":
                        n = st[1]
                        l, bb, t, gi = tile_of(n)
                        sp.wait_ge(s_va, n + 1)
                        sp.wait_ge(done["pv"], max(0, n - NT + 1))
                        sp.dma_start(ve[0:WIN, t, :, :], va[0:WIN, t, :, :]).then_inc(s_ve[t], 16)
                        if t + 1 < NT:
                            sp.wait_ge(done["pv"], max(0, n - NT + 2))
                            sp.dma_start(ve[WIN:P, t + 1, :, :], va[WIN:P, t, :, :]).then_inc(s_ve[t + 1], 16)
                    elif kind == "yT":
                        bb = st[1]
                        sp.wait_ge(s_yo, bb + 1)
                        sp.dma_start(out[turn * NB + bb].rearrange("(t p) d -> p t d", p=P),
                                         yo[:, bb, :, :]).then_inc(s_out[bb], 16)
                for bb in range(NB):
                    sp.wait_ge(s_out[bb], 16)
                sp.wait_ge(s_over, 4)
                sp.sem_clear(of_a_turn)
                for go in (go_pool, go_act, go_dve, go_pe):
                    sp.drain().then_inc(go, 1)

        @block.gpsimd
        def _(pool):
            pool.memset(WoE[:, :, :], 0.0).then_inc(s_wclr, 1)
            pool.memset(mhalf[:, :], -0.5).then_inc(s_pset, 1)
            pool.memset(hT[:, :, 0:1], 0.0).then_inc(s_pset, 1)
            pool.memset(kT[:, :, NT + 1, :], 0.0).then_inc(s_pset, 1)
            pool.memset(ve[:, 0, :, :], 0.0).then_inc(s_pset, 1)
            pool.memset(mv[:, :, :, :, MD:32], 1.0).then_inc(s_pset, 1)
            pool.memset(mm3[:, :, :], 0.0).then_inc(s_mm3, 1)
            pool.wait_ge(s_pset, N_PSET)
            for b in range(B):
                pool.wait_ge(s_vpe, b + 1)
                pool.tensor_tensor(rsx[:, b, :], vpe[:, b, :], mhalf[:, 0:NT], ALU.pow).then_inc(s_rsx, 1)
            pool.wait_ge(s_rope, 16 * len(loads_rope))
            for l in range(DEPTH):
                rope_tables(pool, l)
            pool.wait_ge(s_rsx, B)
            pool.wait_ge(s_mm3, 1)
            pool.wait_ge(s_tab, N_TAB)
            pool.memset(stk[KS:P, :, :, :].rearrange("p b h n -> p (b h n)").bitcast(F32), two_ones)\
                .then_inc(s_ones, 1)
            pool.wait_ge(s_ones, 1)
            with pool.Fori(0, TURNS) as turn:
                for st in steps:
                    kind = st[0]
                    if kind == "sums":
                        n = st[1]
                        for w in range(2):
                            hs = slice(FH * w, FH * w + FH)
                            pool.wait_ge(s_ssc, 2 * n + w + 1)
                            pool.tensor_tensor(rn[:, n % 2, hs], ssc[:, n % 2, hs], mhalf[:, 0:FH], ALU.pow)\
                                .then_inc(s_rn, 1)
                    elif kind == "norm":
                        n = st[1]
                        pool.wait_ge(s_tab, N_TAB)
                        l, bb, t, gi = tile_of(n)
                        for w in range(2):
                            pool.wait_ge(s_qkn, 2 * n + w + 1)
                            pool.wait_ge(s_qk, max(0, 2 * n + w - 1))
                            hs = slice(FH * w, FH * w + FH)
                            for hf in range(2):
                                lo, hi = 32 * hf, 32 * (1 - hf)
                                pool.tensor_tensor(
                                    rs[:, hs, lo:lo + 32], qkn[:, hs, hi:hi + 32],
                                    rt[:, l, 2 * w + 1, t:t + 1, lo:lo + 32].to_broadcast([P, FH, 32]),
                                    ALU.mult).then_inc(s_rs, 1)
                    elif kind == "rope":
                        n = st[1]
                        for w in range(2):
                            hs = slice(FH * w, FH * w + FH)
                            pool.wait_ge(s_rs, 4 * n + 2 * w + 2)
                            pool.wait_ge(s_rc, 2 * n + w + 1)
                            pool.tensor_tensor(qk[:, hs, :], qk[:, hs, :], rs[:, hs, :], ALU.add)\
                                .then_inc(s_qk, 1)
                    elif kind == "rstd":
                        gi = st[1]
                        pool.wait_ge(s_vl, gi + 1)
                        pool.wait_ge(done["rstd"], gi)
                        pool.tensor_tensor(rl[:, :], vl[:, :], mhalf[:, 0:NT], ALU.pow).then_inc(s_rl, 1)
                    elif kind == "mean":
                        gi = st[1]
                        bb = GROUPS[gi][1]
                        pool.wait_ge(s_hc, gi + 1)
                        pool.wait_ge(done["var"], gi)
                        pool.tensor_tensor(hq[:, :], hc[:, :], hc[:, :], ALU.mult).then_inc(s_hq, 1)
                    elif kind == "mscale":
                        _, bb, g = st
                        k = 2 * bb + g
                        pool.wait_ge(s_mrec, k + 1)
                        pool.tensor_tensor(oraw[:, g, :], oraw[:, g, :], mrec[:, :], ALU.mult).then_inc(s_on, 1)
                turn_ends(pool, go_pool)

        @block.scalar
        def _(act):
            for b in range(NB):
                act.dma_start(xtok[:, b, :, :], x[b].rearrange("(t p) d -> p t d", p=P)).then_inc(s_x[b], 16)
            for dst, src in loads_main:
                act.dma_start(dst, src).then_inc(s_main, 16)
            for b in range(NB, B):
                act.dma_start(xtok[:, b, :, :], x[b].rearrange("(t p) d -> p t d", p=P)).then_inc(s_x[b], 16)
            for dst, src in loads_rope:
                act.dma_start(dst, src).then_inc(s_rope, 16)

            act.wait_ge(s_pset, N_PSET)
            act.wait_ge(s_bq0, 1)

            def shift(bb, s):
                act.activation(hT[0:64, bb, :], xT[0:64, bb, :], ACT.Copy).then_inc(s, 1)
                act.activation(hT[64:P, bb, 1:T], xT[64:P, bb, 0:T - 1], ACT.Copy).then_inc(s, 1)

            with act.Fori(0, TURNS) as turn:
                act.activation(wake[:, :], mhalf[:, 0:1], ACT.Exp).then_inc(s_wake, 1)
                for st in steps:
                    kind = st[0]
                    if kind == "hT":
                        l, bb = st[1:]
                        act.wait_ge(s_xT, NB * l + bb + 1)
                        if l:
                            act.wait_ge(s_hc, NB * (l - 1) + bb + 1)
                        shift(bb, s_hT)
                    elif kind == "h2":
                        gi = st[1]
                        bb = GROUPS[gi][1]
                        act.wait_ge(s_x1, gi + 1)
                        act.wait_ge(done["qkv"], 3 * NT * (gi + 1))
                        shift(bb, s_hs)
                    elif kind == "mqkv":
                        bb = st[1]
                        for w in range(2):
                            act.wait_ge(*filled(st, w))
                            src = bank(st, w)
                            act.activation(part[:, bb, w, 0, :], src, ACT.Copy).then_inc(s_p0, 1)
                        act.wait_ge(*filled(st, 2))
                        src = bank(st, 2)
                        act.activation(mv[:, bb, :, :, 0:MD],
                                           src.rearrange("p (t h d) -> p t h d", t=NT, h=MH), ACT.Copy)\
                            .then_inc(s_mv, 1)
                    elif kind == "ropeT":
                        n = st[1]
                        l, bb, t, gi = tile_of(n)
                        act.wait_ge(*filled(st, 0))
                        src = bank(st, 0).rearrange("p (c w i) -> p c w i", c=NP, w=2)
                        act.wait_ge(done["score"], max(0, 2 * (n - 1)))
                        act.activation(bdq[0:64, n % 2, :, :, 0, :], src[0:64], ACT.Copy).then_inc(s_bdq, 1)
                        act.activation(bdq[64:P, n % 2, :, :, 1, :], src[64:P], ACT.Copy).then_inc(s_bdq, 1)
                        act.wait_ge(*filled(st, 1))
                        src = bank(st, 1)
                        act.wait_ge(done["score"], 2 * min(n, NT * gi))
                        act.activation(kT[:, :, t + 1:t + NT + 3:NT + 1, :],
                                       src.rearrange("p (c w i) -> p c w i", c=NP, w=2), ACT.Copy)\
                            .then_inc(s_kT, 1)
                    elif kind == "qkv":
                        n = st[1]
                        l, bb, t, gi = tile_of(n)
                        for w in range(2):
                            act.wait_ge(*filled(st, w))
                            src = bank(st, w)
                            act.wait_ge(s_ss, max(0, 2 * n + w - 1))
                            act.activation(sq[:, FH * w:FH * w + FH, :],
                                               src.rearrange("p (h d) -> p h d", h=FH), ACT.Square)\
                                .then_inc(s_sq, 1)
                        act.wait_ge(*filled(st, 2))
                        src = bank(st, 2)
                        act.wait_ge(done["pv"], max(0, n - NT + 1))
                        act.wait_ge(s_ve[t], 16 * (2 if t else 1) * gi)
                        if t + 1 < NT:
                            act.wait_ge(s_ve[t + 1], 16 * 2 * gi)
                        act.activation(va[:, t, :, 0:FD], src.rearrange("p (h d) -> p h d", h=FH),
                                           ACT.Copy).then_inc(s_va, 1)
                    elif kind == "exp":
                        n = st[1]
                        b = n % 2
                        act.wait_ge(done["wT"], 2 * n)
                        for w in range(2):
                            act.wait_ge(s_wmx, 2 * n + w + 1)
                            src = bank(("score", n), w)
                            for c in range(NP):
                                k = NP * w + c
                                act.activation(pw[:, w, c, :], src[:, P * c:P * c + P], ACT.Exp,
                                               bias=wmx[:, b, k:k + 1], accum_out=wsum[:, b, k:k + 1])\
                                    .then_inc(s_pw, 1)
                    elif kind == "wT":
                        n = st[1]
                        for w in range(2):
                            act.wait_ge(*filled(st, w))
                            src = bank(st, w)
                            act.wait_ge(done["pv"], n)
                            act.activation(pT[:, w, :, :, :],
                                           src.rearrange("p (c a i) -> p c a i", c=NP, a=2), ACT.Copy)\
                                .then_inc(s_pT, 1)
                    elif kind == "pv":
                        n = st[1]
                        l, bb, t, gi = tile_of(n)
                        act.wait_ge(*filled(st, 0))
                        src = bank(st, 0)
                        act.wait_ge(done["wo"], gi)
                        act.activation(oT[:, :, P * t:P * t + P],
                                       src.rearrange("p (c i) -> p c i", c=NP), ACT.Copy).then_inc(s_oT, 1)
                    elif kind == "mlp":
                        gi = st[1]
                        l, bb = GROUPS[gi]
                        act.wait_ge(s_rest, 16 * len(loads_rest))
                        for c, (c0, r) in enumerate(CH):
                            act.wait_ge(*filled(st, 2 * c))
                            src = bank(st, 2 * c)
                            act.wait_ge(done["mlp"], (2 * NCH + 1) * gi)
                            k = 3 + NCH + c
                            act.activation(gl[0:r, c, :], src[0:r], ACT.Gelu, bias=col[0:r, l, k:k + 1])\
                                .then_inc(s_gl, 1)
                        act.wait_ge(s_wake, gi + 1)
                        act.activation(wake[:, :], mhalf[:, 0:1], ACT.Exp).then_inc(s_wake, 1)
                    elif kind == "mexp":
                        _, bb, g, k = st
                        hs, J = exp_units(g)[k]
                        wd = len(hs) * (T - P * J)
                        act.wait_ge(*filled(st, 0))
                        src = bank(st, 0)
                        act.wait_ge(s_mpv, NT * (2 * bb + g) + (k >= NPM))
                        act.activation(pm[:, k % NPM, 0:wd], src[:, 0:wd], ACT.Exp).then_inc(s_pm, 1)
                    elif kind == "mmaxT":
                        bb = st[1]
                        act.wait_ge(*filled(st, 0))
                        src = bank(st, 0)[:, 0:P // 2].bitcast(BF16)
                        act.activation(mmT[:, bb, :], src, ACT.Copy).then_inc(s_mmT, 1)
                    elif kind == "mout":
                        bb = st[1]
                        act.wait_ge(*filled(st, 0))
                        src = bank(st, 0)
                        act.activation(aT[:, bb, :], src, ACT.Copy).then_inc(s_aT, 1)
                turn_ends(act, go_act)

        @block.vector
        def _(dve):
            dve.memset(bdq[:, :, :, :, :, :], 0.0).then_inc(s_bq0, 1)
            def x_stats(b):
                dve.wait_ge(s_x[b], 16)
                for t in range(NT):
                    dve.bn_stats(bst[:, b, t, :], xtok[:, b, t, :]).then_inc(s_st, 1)
                dve.wait_ge(s_st, NT * (b + 1))
                for t in range(NT):
                    dve.bn_aggr(bag[:, b, t, :], bst[:, b, t, :]).then_inc(s_ag, 1)
                dve.wait_ge(s_ag, NT * (b + 1))
                dve.tensor_scalar(vpe[:, b, :], bag[:, b, :, 1], EPS, None, ALU.add).then_inc(s_vpe, 1)

            for b in range(NB):
                x_stats(b)
            dve.wait_ge(s_first, 16 * len(loads_first))
            dve.wait_ge(s_main, 16 * len(loads_main))
            dve.tensor_copy(cb[:, 0:CAUS, :], cf[:, :, :]).then_inc(s_dset, 1)
            dve.tensor_copy(cb[:, CAUS:N_CONST, :], staged).then_inc(s_dset, 1)
            wk = Wm[:, D:2 * D].rearrange("p (h d) -> p h d", h=MH)
            wk2 = Wk2[:, :].rearrange("p (h d) -> p h d", h=MH)
            dve.tensor_tensor(wdot[:, :, :], wk[:, :, 0:3], dirs[:, :, :], ALU.mult).then_inc(s_dset, 1)
            dve.wait_ge(s_dset, 3)
            dve.tensor_reduce(wgeo[:, 0, :], wdot[:, :, :], AX.X, ALU.add).then_inc(s_dset, 1)
            dve.wait_ge(s_dset, 4)
            dve.tensor_tensor(wgeo[:, 1, :], wgeo[:, 0, :], hsc[:, :], ALU.mult).then_inc(s_dset, 1)
            dve.wait_ge(s_dset, 5)
            dve.tensor_tensor(wgd[:, :, :], dirs[:, :, :],
                                  wgeo[:, 1, :].rearrange("p (h a) -> p h a", a=1).to_broadcast([P, MH, 3]),
                                  ALU.mult).then_inc(s_dset, 1)
            dve.tensor_scalar(Wk2[:, :], Wm[:, D:2 * D], float(MD) ** -0.5, None, ALU.mult).then_inc(s_dset, 1)
            dve.wait_ge(s_dset, 7)
            dve.tensor_tensor(wk2[:, :, 0:3], wk2[:, :, 0:3], wgd[:, :, :], ALU.add).then_inc(s_dset, 1)
            for b in range(NB, B):
                x_stats(b)
            dve.wait_ge(s_mm3, 1)

            def split(src, p0, rest_, p1, p2, s, n):
                dve.tensor_copy(p0, src).then_inc(s, 1)
                dve.wait_ge(s, n + 1)
                dve.tensor_tensor(rest_, src, p0, ALU.subtract).then_inc(s, 1)
                dve.wait_ge(s, n + 2)
                dve.tensor_copy(p1, rest_).then_inc(s, 1)
                dve.wait_ge(s, n + 3)
                dve.tensor_tensor(p2, rest_, p1, ALU.subtract).then_inc(s, 1)

            with dve.Fori(0, TURNS) as turn:
                for st in steps:
                    kind = st[0]
                    if kind == "xT":
                        bb = st[1]
                        if bb == 0:
                            dve.wait_ge(s_rsx, B)
                            first = turn * NB
                            dve.tensor_copy(lnx[:, 0, :, :], bag[:, bass.ds(first, NB), :, 0]).then_inc(s_ln, 1)
                            dve.tensor_copy(lnx[:, 1, :, :], rsx[:, bass.ds(first, NB), :]).then_inc(s_ln, 1)
                            dve.wait_ge(s_ln, 2)
                        for t in range(NT):
                            dve.tensor_scalar(xn[:, bb, t, :], xtok[:, bass.ds(turn * NB + bb, 1), t, :],
                                              lnx[:, 0, bb, t:t + 1], lnx[:, 1, bb, t:t + 1],
                                              ALU.subtract, ALU.mult).then_inc(s_xn, 1)
                        dve.wait_ge(*filled(st, 0))
                        src = bank(st, 0)
                        dve.tensor_copy(xT[:, bb, :], src).then_inc(s_xT, 1)
                    elif kind == "mqkv":
                        bb = st[1]
                        for w in range(2):
                            i = 2 * bb + w
                            dve.wait_ge(*filled(st, w))
                            src = bank(st, w)
                            dve.wait_ge(s_p0, i + 1)
                            dve.wait_ge(s_p2, max(0, i - 1))
                            dve.tensor_tensor(rest[:, w, :], src, part[:, bb, w, 0, :], ALU.subtract)\
                                .then_inc(s_re, 1)
                            dve.wait_ge(s_re, i + 1)
                            dve.tensor_copy(part[:, bb, w, 1, :], rest[:, w, :]).then_inc(s_p1, 1)
                            dve.wait_ge(s_p1, i + 1)
                            dve.tensor_tensor(part[:, bb, w, 2, :], rest[:, w, :], part[:, bb, w, 1, :],
                                                  ALU.subtract).then_inc(s_p2, 1)
                    elif kind == "sums":
                        n = st[1]
                        b = n % 2
                        for w in range(2):
                            hs = slice(FH * w, FH * w + FH)
                            dve.wait_ge(s_sq, 2 * n + w + 1)
                            dve.tensor_reduce(ss[:, b, hs], sq[:, hs, :], AX.X, ALU.add).then_inc(s_ss, 1)
                            dve.wait_ge(s_ss, 2 * n + w + 1)
                            dve.tensor_scalar(ssc[:, b, hs], ss[:, b, hs], 1e-24, None, ALU.max)\
                                .then_inc(s_ssc, 1)
                    elif kind == "norm":
                        n = st[1]
                        b = n % 2
                        for w in range(2):
                            hs = slice(FH * w, FH * w + FH)
                            src = bank(("qkv", n), w).rearrange("p (h d) -> p h d", h=FH)
                            dve.wait_ge(s_rn, 2 * n + w + 1)
                            dve.wait_ge(s_rs, max(0, 4 * (n - 1)))
                            dve.tensor_tensor(
                                qkn[:, hs, :], src,
                                rn[:, b, hs].rearrange("p (h a) -> p h a", a=1).to_broadcast([P, FH, FD]),
                                ALU.mult).then_inc(s_qkn, 1)
                    elif kind == "rope":
                        n = st[1]
                        l, bb, t, gi = tile_of(n)
                        dve.wait_ge(s_tab, N_TAB)
                        for w in range(2):
                            hs = slice(FH * w, FH * w + FH)
                            dve.wait_ge(s_qkn, 2 * n + w + 1)
                            dve.wait_ge(done["ropeT"], max(0, 2 * n + w - 1))
                            dve.tensor_tensor(
                                qk[:, hs, :], qkn[:, hs, :],
                                rt[:, l, 2 * w, t:t + 1, :].to_broadcast([P, FH, FD]), ALU.mult)\
                                .then_inc(s_rc, 1)
                    elif kind == "score":
                        n = st[1]
                        b = n % 2
                        for w in range(2):
                            dve.wait_ge(*filled(st, w))
                            src = bank(st, w).rearrange("p (c j) -> p c j", c=NP)
                            dve.wait_ge(s_pw, max(0, 2 * NP * (n - 1)))
                            dve.tensor_reduce(wmx[:, b, NP * w:NP * w + NP], src, AX.X, ALU.max,
                                              negate=True).then_inc(s_wmx, 1)
                    elif kind == "weights":
                        n = st[1]
                        b = n % 2
                        for w in range(2):
                            ks = slice(NP * w, NP * w + NP)
                            dve.wait_ge(s_pw, NP * (2 * n + w + 1))
                            dve.wait_ge(s_wn, max(0, 2 * n + w - 3))
                            dve.reciprocal(wrec[:, b, ks], wsum[:, b, ks]).then_inc(s_wrec, 1)
                            dve.wait_ge(s_wrec, 2 * n + w + 1)
                            dve.tensor_tensor(
                                pw[:, w, :, :], pw[:, w, :, :],
                                wrec[:, b, ks].rearrange("p (c a) -> p c a", a=1).to_broadcast([P, NP, P]),
                                ALU.mult).then_inc(s_wn, 1)
                    elif kind == "wo":
                        gi = st[1]
                        l, bb = GROUPS[gi]
                        dve.wait_ge(*filled(st, 0))
                        src = bank(st, 0)
                        dve.wait_ge(s_hT, 2 * (NB * l + bb) + 2)
                        dve.wait_ge(done["mqkv"], 3 * NB)
                        dve.tensor_tensor(xT[:, bb, :], src, xT[:, bb, :], ALU.add).then_inc(s_x1, 1)
                    elif kind == "mean":
                        gi = st[1]
                        bb = GROUPS[gi][1]
                        dve.wait_ge(*filled(st, 0))
                        src = bank(st, 0)
                        dve.wait_ge(done["mlp"], (2 * NCH + 1) * gi)
                        dve.tensor_tensor(hc[:, :], hT[:, bb, :], src, ALU.subtract).then_inc(s_hc, 1)
                    elif kind == "var":
                        gi = st[1]
                        dve.wait_ge(*filled(st, 0))
                        src = bank(st, 0)
                        dve.wait_ge(s_rl, gi)
                        dve.tensor_scalar(vl[:, :], src[:, 0:NT], EPS, None, ALU.add).then_inc(s_vl, 1)
                    elif kind == "rstd":
                        gi = st[1]
                        l, bb = GROUPS[gi]
                        dve.wait_ge(*filled(st, 0))
                        src = bank(st, 0)
                        dve.wait_ge(s_hq, gi + 1)
                        dve.wait_ge(s_rest, 16 * len(loads_rest))
                        dve.tensor_tensor(hc[:, :], hc[:, :], src, ALU.mult).then_inc(s_hu, 1)
                        dve.wait_ge(s_hu, gi + 1)
                        dve.tensor_scalar(hc[:, :], hc[:, :], col[:, l, 0:1], col[:, l, 1:2],
                                          ALU.mult, ALU.add).then_inc(s_hn, 1)
                    elif kind == "mlp":
                        gi = st[1]
                        l, bb = GROUPS[gi]
                        for c, (c0, r) in enumerate(CH):
                            dve.wait_ge(*filled(st, 2 * c + 1))
                            src = bank(st, 2 * c + 1)
                            dve.wait_ge(s_gl, NCH * gi + c + 1)
                            dve.scalar_tensor_tensor(out=gl[0:r, c, :], in0=src[0:r],
                                                         scalar=col[0:r, l, 3 + c:4 + c], in1=gl[0:r, c, :],
                                                         op0=ALU.add, op1=ALU.mult).then_inc(s_uu, 1)
                        dve.wait_ge(*filled(st, 2 * NCH))
                        src = bank(st, 2 * NCH)
                        dve.wait_ge(s_hs, 2 * gi + 2)
                        dve.scalar_tensor_tensor(out=xT[:, bb, :], in0=src, scalar=col[:, l, 2:3],
                                                     in1=xT[:, bb, :], op0=ALU.add, op1=ALU.add)\
                            .then_inc(s_xT if l + 1 < DEPTH else s_y1, 1)
                    elif kind == "mmax":
                        _, bb, g, k = st
                        hs, I = max_units(g)[k]
                        wd = P * (I + 1)
                        dve.wait_ge(*filled(st, 0))
                        src = bank(st, 0)[:, 0:len(hs) * wd].rearrange("p (h j) -> p h j", j=wd)
                        dve.tensor_reduce(mmx[:, bb, I, hs[0]:hs[-1] + 1], src, AX.X, ALU.max,
                                              negate=True).then_inc(s_mmx, 1)
                    elif kind == "mmaxT":
                        bb = st[1]
                        dve.wait_ge(s_mmx, 2 * NU * (bb + 1))
                        k = NT * MH
                        split(mmx[:, bb, :, :].rearrange("p i h -> p (i h)"), mm3[:, bb, 0:k],
                              mmr[:, bb, :], mm3[:, bb, k:2 * k], mm3[:, bb, 2 * k:3 * k], s_mm, 4 * bb)
                    elif kind == "mcopy":
                        _, bb, g = st
                        k = 2 * bb + g
                        dve.wait_ge(s_mpv, NT * (k + 1))
                        dve.wait_ge(done["mout"], bb)
                        dve.tensor_copy(oraw[:, g, :], acc[:, :]).then_inc(s_or, 1)
                    elif kind == "mden":
                        _, bb, g = st
                        k = 2 * bb + g
                        dve.wait_ge(*filled(st, 0))
                        src = bank(st, 0)
                        dve.wait_ge(s_on, k)
                        dve.reciprocal(mrec[:, :], src).then_inc(s_mrec, 1)
                    elif kind == "yT":
                        bb = st[1]
                        dve.wait_ge(s_aT, bb + 1)
                        dve.wait_ge(s_y1, bb + 1)
                        dve.tensor_tensor(aT[:, bb, :], xT[:, bb, :], aT[:, bb, :], ALU.add).then_inc(s_yT, 1)
                        dve.wait_ge(*filled(st, 0))
                        src = bank(st, 0)
                        dve.tensor_tensor(yo[:, bb, :, :].rearrange("p t d -> p (t d)"), src,
                                              xtok[:, bass.ds(turn * NB + bb, 1), :, :]
                                              .rearrange("p b t d -> p (b t d)"), ALU.add)\
                            .then_inc(s_yo, 1)
                turn_ends(dve, go_dve)

        @block.tensor
        def _(pe):
            pe.wait_ge(s_dset, N_DSET)

            def mm(o, a, b, start=True, stop=True):
                return pe.matmul(o, a, b, start=start, stop=stop)

            with pe.Fori(0, TURNS) as turn:
                for st in steps:
                    kind = st[0]
                    if kind == "xT":
                        bb = st[1]
                        pe.wait_ge(*emptied(st, 0))
                        o = bank(st, 0)
                        pe.wait_ge(s_xn, NT * (bb + 1))
                        for t in range(NT):
                            i = pe.transpose(o[:, P * t:P * t + P], xn[:, bb, t, :], identf)
                        i.then_inc(done[kind], 1)
                    elif kind == "mqkv":
                        bb = st[1]
                        pe.wait_ge(s_xT, bb + 1)
                        pe.wait_ge(*emptied(st, 0))
                        mm(bank(st, 0), Wm[:, 0:D], xT[:, bb, :]).then_inc(done[kind], 1)
                        pe.wait_ge(*emptied(st, 1))
                        mm(bank(st, 1), Wk2[:, :], xT[:, bb, :]).then_inc(done[kind], 1)
                        pe.wait_ge(*emptied(st, 2))
                        o = bank(st, 2)
                        for t in range(NT):
                            i = mm(o[:, P * t:P * t + P], xT[:, bb, P * t:P * t + P], Wm[:, 2 * D:3 * D])
                        i.then_inc(done[kind], 1)
                    elif kind == "qkv":
                        n = st[1]
                        l, bb, t, gi = tile_of(n)
                        if n == 0:
                            pe.wait_ge(s_wf, 16)
                        if n == NT * NB:
                            pe.wait_ge(s_rest, 16 * len(loads_rest))
                        pe.wait_ge(s_hT, 2 * (NB * l + bb) + 2)
                        for w in range(3):
                            pe.wait_ge(*emptied(st, w))
                            o = bank(st, w)
                            mm(o, hT[:, bb, P * t:P * t + P], Wf[:, l, INNER * w:INNER * (w + 1)])\
                                .then_inc(done[kind], 1)
                    elif kind == "ropeT":
                        n = st[1]
                        for w in range(2):
                            pe.wait_ge(s_qk, 2 * n + w + 1)
                            pe.wait_ge(*emptied(st, w))
                            o = bank(st, w)
                            for c in range(NP):
                                h = FH * w + 2 * c
                                i = pe.transpose(o[:, P * c:P * c + P],
                                                 qk[:, h:h + 2, :].rearrange("p h d -> p (h d)"), identf)
                            i.then_inc(done[kind], 1)
                    elif kind == "score":
                        n = st[1]
                        l, bb, t, gi = tile_of(n)
                        pe.wait_ge(s_bdq, 2 * n + 2)
                        pe.wait_ge(s_kT, n + 1)
                        for w in range(2):
                            pe.wait_ge(*emptied(st, w))
                            o = bank(st, w)
                            m = WIN1 if w else (WINE if t else WIN0)
                            mm(o, identb, cb[:, m:m + 1, :].to_broadcast([P, NP, P]), True, False)
                            other = NT + 1 if w else NT
                            for c in range(NP):
                                i = mm(o[:, P * c:P * c + P].rearrange("p (b j) -> p b j", b=2),
                                       bdq[:, n % 2, c, w, :, :].rearrange("p a i -> p (a i)"),
                                       kT[:, c, t + 1:t + other + 2:other, :], False, c == NP - 1)
                            i.then_inc(done[kind], 1)
                    elif kind == "wT":
                        n = st[1]
                        for w in range(2):
                            pe.wait_ge(*emptied(st, w))
                            o = bank(st, w)
                            pe.wait_ge(s_wn, 2 * n + w + 1)
                            for c in range(NP):
                                i = pe.transpose(o[:, P * c:P * c + P], pw[:, w, c, :], identf)
                            i.then_inc(done[kind], 1)
                    elif kind == "pv":
                        n = st[1]
                        l, bb, t, gi = tile_of(n)
                        pe.wait_ge(s_pT, 2 * n + 2)
                        pe.wait_ge(s_va, n + 1)
                        pe.wait_ge(s_ve[t], 16 * (2 if t else 1) * (gi + 1))
                        pe.wait_ge(*emptied(st, 0))
                        o = bank(st, 0)
                        for c in range(NP):
                            for w, v in ((0, ve), (1, va)):
                                for a in range(2):
                                    i0 = P * c + WIN * w
                                    i = mm(o[FD * a:FD * a + FD, i0:i0 + WIN], v[:, t, 2 * c + a, :],
                                           pT[:, w, c, a, :])
                        i.then_inc(done[kind], 1)
                    elif kind == "wo":
                        gi = st[1]
                        l, bb = GROUPS[gi]
                        pe.wait_ge(*emptied(st, 0))
                        o = bank(st, 0)
                        pe.wait_ge(s_oT, NT * (gi + 1))
                        pe.wait_ge(s_rest, 16 * len(loads_rest))
                        for c in range(NP):
                            i = mm(o, Wo[:, l, c, :], oT[:, c, :], c == 0, c == NP - 1)
                        i.then_inc(done[kind], 1)
                    elif kind == "mean":
                        gi = st[1]
                        bb = GROUPS[gi][1]
                        pe.wait_ge(*emptied(st, 0))
                        o = bank(st, 0)
                        pe.wait_ge(s_hs, 2 * gi + 2)
                        mm(o, cf[:, MEAN, :], hT[:, bb, :]).then_inc(done[kind], 1)
                    elif kind == "var":
                        gi = st[1]
                        pe.wait_ge(*emptied(st, 0))
                        o = bank(st, 0)
                        pe.wait_ge(s_hq, gi + 1)
                        for t in range(NT):
                            i = mm(o[:, t:t + 1], hq[:, P * t:P * t + P], cf[:, MEAN, 0:1])
                        i.then_inc(done[kind], 1)
                    elif kind == "rstd":
                        gi = st[1]
                        pe.wait_ge(*emptied(st, 0))
                        o = bank(st, 0)
                        pe.wait_ge(s_rl, gi + 1)
                        for t in range(NT):
                            i = mm(o[:, P * t:P * t + P], rl[:, t:t + 1].to_broadcast([P, P]), identf)
                        i.then_inc(done[kind], 1)
                    elif kind == "mlp":
                        gi = st[1]
                        l, bb = GROUPS[gi]
                        pe.wait_ge(s_hn, gi + 1)
                        pe.wait_ge(s_rest, 16 * len(loads_rest))
                        for c, (c0, r) in enumerate(CH):
                            for i, first in ((0, HID + c0), (1, c0)):
                                pe.wait_ge(*emptied(st, 2 * c + i))
                                o = bank(st, 2 * c + i)
                                mm(o[0:r], W1[:, l, first:first + r], hc[:, :]).then_inc(done[kind], 1)
                        pe.wait_ge(*emptied(st, 2 * NCH))
                        o = bank(st, 2 * NCH)
                        for c, (c0, r) in enumerate(CH):
                            pe.wait_ge(s_uu, NCH * gi + c + 1)
                            i = mm(o, W2[0:r, l, c, :], gl[0:r, c, :], c == 0, c == NCH - 1)
                        i.then_inc(done[kind], 1)
                    elif kind == "mmax":
                        _, bb, g, k = st
                        hs, I = max_units(g)[k]
                        wd = P * (I + 1)
                        pe.wait_ge(*emptied(st, 0))
                        o = bank(st, 0)
                        pe.wait_ge(s_stk[bb], 16 * 2 * len(TERMS))
                        for j, h in enumerate(hs):
                            mm(o[:, wd * j:wd * (j + 1)], stq[0:KS, bb, h, P * I:P * I + P],
                               stk[0:KS, bb, h, 0:wd], True, False)
                            i = mm(o[:, wd * j + P * I:wd * (j + 1)], identb, cb[:, CAUS, :], False, True)
                        i.then_inc(done[kind], 1)
                    elif kind == "mmaxT":
                        bb = st[1]
                        pe.wait_ge(*emptied(st, 0))
                        o = bank(st, 0)
                        pe.wait_ge(s_mm, 4 * bb + 4)
                        pe.transpose(o[:, 0:P // 2].bitcast(BF16), mm3[:, bb, :], identb)\
                            .then_inc(done[kind], 1)
                    elif kind == "mexp":
                        _, bb, g, k = st
                        hs, J = exp_units(g)[k]
                        wd = T - P * J
                        pe.wait_ge(*emptied(st, 0))
                        o = bank(st, 0)
                        pe.wait_ge(s_mst[bb], 16 * 3 * NT)
                        pe.wait_ge(s_ones, 1)
                        for j, h in enumerate(hs):
                            mm(o[:, wd * j:wd * (j + 1)], stk[0:KM, bb, h, P * J:P * J + P],
                               stq[0:KM, bb, h, P * J:T], True, False)
                            i = mm(o[:, wd * j:wd * j + P], identb, cb[:, CAUST, :], False, True)
                        i.then_inc(done[kind], 1)
                    elif kind == "mpv":
                        _, bb, g, J = st
                        wd = T - P * J
                        n = 2 * bb + g
                        pe.wait_ge(s_mv, bb + 1)
                        if J == 0:
                            pe.wait_ge(s_or, n)
                        for k in UNITS_OF_J[J]:
                            pe.wait_ge(s_pm, NU * n + k + 1)
                        for k in UNITS_OF_J[J]:
                            for j, h in enumerate(exp_units(g)[k][0]):
                                p0 = 32 * (h % GH)
                                i = mm(acc[p0:p0 + 32, P * J:T], mv[:, bb, J, h, :],
                                       pm[:, k % NPM, wd * j:wd * (j + 1)], J == 0, J == NT - 1)
                        i.then_inc(s_mpv, 1)
                    elif kind == "mden":
                        _, bb, g = st
                        pe.wait_ge(*emptied(st, 0))
                        o = bank(st, 0)
                        pe.wait_ge(s_or, 2 * bb + g + 1)
                        mm(o, cf[:, DEN, :], oraw[:, g, :]).then_inc(done[kind], 1)
                    elif kind == "mout":
                        bb = st[1]
                        pe.wait_ge(*emptied(st, 0))
                        o = bank(st, 0)
                        pe.wait_ge(s_on, 2 * bb + 2)
                        pe.wait_ge(s_rest, 16 * len(loads_rest))
                        for g in range(2):
                            i = mm(o, WoE[:, g, :], oraw[:, g, :], g == 0, g == 1)
                        i.then_inc(done[kind], 1)
                    elif kind == "yT":
                        bb = st[1]
                        pe.wait_ge(*emptied(st, 0))
                        o = bank(st, 0)
                        pe.wait_ge(s_yT, bb + 1)
                        for t in range(NT):
                            i = pe.transpose(o[:, P * t:P * t + P], aT[:, bb, P * t:P * t + P], identf)
                        i.then_inc(done[kind], 1)
                turn_ends(pe, go_pe)


_INS = ["L0_attn_x", "L0_attn_Wqkv", "L0_attn_Wout", "L0_attn_head_scales", "L0_attn_head_dirs", "L0_ffn_wqkv",
        "L0_ffn_q_scale", "L0_ffn_k_scale", "L0_ffn_wo", "L0_ffn_ln_g", "L0_ffn_ln_b", "L0_ffn_w1", "L0_ffn_b1",
        "L0_ffn_w2", "L0_ffn_b2"]


def kernel(**inputs):
    import numpy as _np
    import concourse.bacc as _bacc
    from concourse import mybir as _mybir
    from concourse.bass_utils import run_bass_kernel_spmd as _run

    nc = _bacc.Bacc("TRN2", target_bir_lowering=False, num_devices=1)
    arrays, args = {}, []
    given = [(n, _np.ascontiguousarray(inputs[n])) for n in _INS] + list(zip(("consts", "rope"), constants()))
    for name, a in given:
        arrays[f"in_{name}_dram"] = a
        args.append(nc.dram_tensor(f"in_{name}_dram", a.shape, _mybir.dt.from_np(a.dtype),
                                   kind="ExternalInput").ap())
    args.append(nc.dram_tensor("out_0_dram", (B, T, D), _mybir.dt.float32, kind="ExternalOutput").ap())
    build(nc, *args)
    r = _run(nc, [arrays], core_ids=[0])
    return r.results[0]["out_0_dram"]
```
